# Optimizing a Trainium2 kernel written in Bass

```python
import numpy as np
import jax
import jax.numpy as jnp

def _softmax(x, axis=-1):
    return jax.nn.softmax(x, axis=axis)
def _gelu(x):
    return jax.nn.gelu(x, approximate=True)
def _silu(x):
    return jax.nn.silu(x)
def _sigmoid(x):
    return jax.nn.sigmoid(x)
def _layernorm(x, axis=-1, eps=1e-5):
    m = jnp.mean(x, axis=axis, keepdims=True)
    v = jnp.var(x, axis=axis, keepdims=True)
    return (x - m) / jnp.sqrt(v + eps)
def _scatter_add(tgt, idx, src, axis=0):
    return tgt.at[idx].add(src)
def _segment_sum(src, seg, n):
    return jax.ops.segment_sum(src, seg, n)

kernel_name = 'mk_conv_preact_d1_conv_nchw256_40c0e1'

def setup_inputs(seed: int = 0):
    np.random.seed(seed)
    _w = jnp.asarray
    def _rec_inputs():
        import jax
        import jax.numpy as jnp
        _gk = jax.random.key(seed)
        x = -0.0003929 + 0.9999 * jax.random.normal(jax.random.fold_in(_gk, 1), (4, 256, 256, 64), jnp.float32)
        return x
    x = _rec_inputs()
    def _L0_conv_setup():
        import jax, jax.numpy as jnp
        import numpy as np
        from jax import lax

        def _dct_mat(N):
            n = np.arange(N)
            k = np.arange(N)[:, None]
            return jnp.asarray(2.0 * np.cos(np.pi * (2 * n + 1) * k / (2 * N)), jnp.float32)

        def _idct_mat(N):
            n = np.arange(N)[:, None]
            k = np.arange(N)
            w = np.ones(N)
            w[0] = 0.5
            return jnp.asarray(w * np.cos(np.pi * (2 * n + 1) * k / (2 * N)) / N, jnp.float32)

        def _l2norm(x, eps=1e-12):
            n = jnp.sqrt(jnp.sum(x * x, axis=-1, keepdims=True))
            return x / jnp.maximum(n, eps)
        key = jax.random.key(seed)
        ks = jax.random.split(key, 10)
        B, H, W, C = (4, 256, 256, 64)
        heads, dim_head = (4, 16)
        hd = heads * dim_head
        s = 0.05
        return {'x_input': jax.random.normal(ks[0], (B, H, W, C), jnp.float32), 'Wq': jax.random.normal(ks[1], (C, hd), jnp.float32) * s, 'Wk': jax.random.normal(ks[2], (C, hd), jnp.float32) * s, 'Wv': jax.random.normal(ks[3], (C, hd), jnp.float32) * s, 'rescale': jnp.ones((heads, 1, 1), jnp.float32), 'proj_w': jax.random.normal(ks[4], (hd, C), jnp.float32) * s, 'proj_b': jnp.zeros((C,), jnp.float32), 'c1a_w': jax.random.normal(ks[5], (C, C, 1, 1), jnp.float32) * s, 'c1b_w': jax.random.normal(ks[6], (C, 1, 3, 3), jnp.float32) * s, 'c2_w': jax.random.normal(ks[7], (C, C, 1, 1), jnp.float32) * s, 'coef_emb': jax.random.uniform(ks[8], (H, W), jnp.float32)}
    _L0_conv_all = _L0_conv_setup()
    _L0_conv_in = {k: v for k, v in _L0_conv_all.items() if k in ('Wq', 'Wk', 'Wv', 'rescale', 'proj_w', 'proj_b', 'c1a_w', 'c1b_w', 'c2_w', 'coef_emb', )}
    del _L0_conv_all

    return {
        "x": x,
        "L0_conv_Wq": _L0_conv_in["Wq"],
        "L0_conv_Wk": _L0_conv_in["Wk"],
        "L0_conv_Wv": _L0_conv_in["Wv"],
        "L0_conv_rescale": _L0_conv_in["rescale"],
        "L0_conv_proj_w": _L0_conv_in["proj_w"],
        "L0_conv_proj_b": _L0_conv_in["proj_b"],
        "L0_conv_c1a_w": _L0_conv_in["c1a_w"],
        "L0_conv_c1b_w": _L0_conv_in["c1b_w"],
        "L0_conv_c2_w": _L0_conv_in["c2_w"],
        "L0_conv_coef_emb": _L0_conv_in["coef_emb"],
    }

def reference(x, L0_conv_Wq, L0_conv_Wk, L0_conv_Wv, L0_conv_rescale, L0_conv_proj_w, L0_conv_proj_b, L0_conv_c1a_w, L0_conv_c1b_w, L0_conv_c2_w, L0_conv_coef_emb):
    import jax
    import jax.numpy as jnp
    def _L0_conv_ref(x_input, Wq, Wk, Wv, rescale, proj_w, proj_b, c1a_w, c1b_w, c2_w, coef_emb):
        import jax, jax.numpy as jnp
        import numpy as np
        from jax import lax

        def _dct_mat(N):
            n = np.arange(N)
            k = np.arange(N)[:, None]
            return jnp.asarray(2.0 * np.cos(np.pi * (2 * n + 1) * k / (2 * N)), jnp.float32)

        def _idct_mat(N):
            n = np.arange(N)[:, None]
            k = np.arange(N)
            w = np.ones(N)
            w[0] = 0.5
            return jnp.asarray(w * np.cos(np.pi * (2 * n + 1) * k / (2 * N)) / N, jnp.float32)

        def _l2norm(x, eps=1e-12):
            n = jnp.sqrt(jnp.sum(x * x, axis=-1, keepdims=True))
            return x / jnp.maximum(n, eps)
        bs, H, W, C = x_input.shape
        K = 8
        hh, ww = (H // K, W // K)
        heads = rescale.shape[0]
        MH, MW = (_dct_mat(H), _dct_mat(W))
        x_in = jnp.transpose(x_input, (0, 3, 1, 2))
        x_dct = jnp.einsum('bchw,kw->bchk', x_in, MW)
        x_dct = jnp.einsum('bchw,kh->bckw', x_dct, MH)
        xb = x_dct.reshape(bs, C, hh, K, ww, K)
        x_tri = jnp.transpose(xb, (0, 2, 4, 3, 5, 1)).reshape(bs, hh * ww, K * K, C)

        def split(t):
            b, n, mm, hd = t.shape
            t = t.reshape(b, n, mm, heads, hd // heads)
            return jnp.transpose(t, (0, 1, 3, 4, 2))
        q = _l2norm(split(x_tri @ Wq))
        k = _l2norm(split(x_tri @ Wk))
        v = split(x_tri @ Wv)
        attn = jnp.einsum('bnhdm,bnhem->bnhde', q, k) * rescale[None, None]
        attn = jax.nn.softmax(attn, axis=-1)
        x0 = jnp.einsum('bnhde,bnhem->bnhdm', attn, v)
        x1 = jnp.transpose(x0, (0, 1, 4, 2, 3)).reshape(bs, hh * ww, K * K, -1)
        x2 = x1 @ proj_w + proj_b
        x3 = x2.reshape(bs, hh, ww, K, K, C)
        x_low = jnp.transpose(x3, (0, 5, 1, 3, 2, 4)).reshape(bs, C, H, W)
        dn = ('NCHW', 'OIHW', 'NCHW')
        g = lambda t: jax.nn.gelu(t, approximate=False)
        h1 = g(lax.conv_general_dilated(x_dct, c1a_w, (1, 1), 'VALID', dimension_numbers=dn))
        h1 = g(lax.conv_general_dilated(h1, c1b_w, (1, 1), ((1, 1), (1, 1)), dimension_numbers=dn, feature_group_count=C))
        x_conv = h1 + x_dct
        h2 = g(lax.conv_general_dilated(x_conv, c2_w, (1, 1), 'VALID', dimension_numbers=dn))
        x_high = h2 + x_conv
        coef = coef_emb[None, None]
        x_out = coef * x_low + (1.0 - coef) * x_high + x_dct
        IH, IW = (_idct_mat(H), _idct_mat(W))
        x_out = jnp.einsum('bchw,nw->bchn', x_out, IW)
        x_out = jnp.einsum('bchw,nh->bcnw', x_out, IH)
        return jnp.transpose(x_out, (0, 2, 3, 1))

    def _gn(v, G=32, eps=1e-5):
        B_, C_, H_, W_ = v.shape
        g = v.reshape(B_, G, C_ // G, H_, W_)
        m = jnp.mean(g, axis=(2, 3, 4), keepdims=True)
        s = jnp.var(g, axis=(2, 3, 4), keepdims=True)
        return ((g - m) / jnp.sqrt(s + eps)).reshape(v.shape)

    def _ln_c(v, eps=1e-6):
        m = jnp.mean(v, axis=1, keepdims=True)
        s = jnp.var(v, axis=1, keepdims=True)
        return (v - m) / jnp.sqrt(s + eps)

    def _ln_t(v, eps=1e-5):
        m = jnp.mean(v, axis=-1, keepdims=True)
        s = jnp.var(v, axis=-1, keepdims=True)
        return (v - m) / jnp.sqrt(s + eps)

    def _to_tokens(v):
        B_, C_, H_, W_ = v.shape
        return v.reshape(B_, C_, H_ * W_).transpose(0, 2, 1)
    def _from_tokens(t, like):
        B_, C_, H_, W_ = like.shape
        return t.transpose(0, 2, 1).reshape(B_, C_, H_, W_)

    x = x + _L0_conv_ref(_gn(x), L0_conv_Wq, L0_conv_Wk, L0_conv_Wv, L0_conv_rescale, L0_conv_proj_w, L0_conv_proj_b, L0_conv_c1a_w, L0_conv_c1b_w, L0_conv_c2_w, L0_conv_coef_emb)
    return x


_drawn_inputs = setup_inputs


def setup_inputs(seed=0):
    import zlib

    import numpy as np

    out = dict(_drawn_inputs(seed))
    spreads = {'L0_conv_rescale': (1.0, 0.6), 'L0_conv_proj_b': (0.0, 0.8)}
    factors = {'L0_conv_Wq': 8.0,
     'L0_conv_Wk': 8.0,
     'L0_conv_Wv': 6.187,
     'L0_conv_proj_w': 6.238,
     'L0_conv_c1a_w': 8.0,
     'L0_conv_c1b_w': 8.0}
    for name, (base, spread) in spreads.items():
        noise = np.random.default_rng([zlib.crc32(name.encode()), seed]).standard_normal(out[name].shape)
        drawn = base * np.exp(spread * noise) if base else spread * noise
        out[name] = jnp.asarray(drawn.astype(out[name].dtype))
    for name, factor in factors.items():
        out[name] = (out[name] * factor).astype(out[name].dtype)
    return out
```

```python
from contextlib import ExitStack

import concourse.bass as bass
from concourse import mybir

F32 = mybir.dt.float32
ALU = mybir.AluOpType
ACT = mybir.ActivationFunctionType
AX = mybir.AxisListType

P = 128
B, H, W, C = 4, 256, 256, 64
GROUP_ROWS = 8
K = 8
HEADS, DH = 4, 16
BANK = 512

COLS = W * C
QUARTERS = 4
QCOLS = COLS // QUARTERS
TILES = QCOLS // BANK
BATCH = 4
F_TILES = 2 * TILES
F_CREDIT = 2 * TILES * QUARTERS
F_BANKS = 4

STRIPS = H // 2 // K
ROWS = K + 2
NB = W // K
T2 = NB // 2
TAPS = 9
ACT_ORDER = ([("dct", j) for j in range(5)] + [("c1", j) for j in range(5)]
             + [("conv", 0), ("conv", 1), ("conv", 2), ("c2", 0), ("conv", 3), ("c2", 1)]
             + [("v", j) for j in range(4)] + [("c2", 2), ("c2", 3)] + [("u", j) for j in range(8)])
DVE_ORDER = ([("qk", j) for j in range(8)] + [("norm", 0)] + [("s", j) for j in range(2)]
             + [("rk", j) for j in range(2)] + [("low", j) for j in range(4)]
             + [("t", j) for j in range(4)] + [("idct", j) for j in range(4)])
ACT_TILES, DVE_TILES = len(ACT_ORDER), len(DVE_ORDER)
ACT_BANKS, DVE_BANKS = 3, 5
ACT_CREDIT = ACT_TILES - 4
assert ACT_TILES % ACT_BANKS == 0 and DVE_TILES % DVE_BANKS == 0

WT = 16
I_STEPS = W // WT // 2


def forward_phase(nc, x, y_dram, dct, group_avg, psum):
    with ExitStack() as ctx:
        def sb(name, shape):
            return ctx.enter_context(nc.sbuf_tensor("f_" + name, shape, F32))

        def sem(name):
            return ctx.enter_context(nc.semaphore("f_" + name))

        x_sb = sb("x_sb", [P, 2, COLS])
        xn = sb("xn", [P, 4, 2, BANK])
        y_sb = sb("y_sb", [P, 2, 2, BATCH * BANK])
        dct_h = sb("dct_h", [P, 2, H])
        avg = sb("avg", [P, P])
        zero_row = sb("zero_row", [P, COLS // P])
        stats = sb("stats", [P, 2, COLS // BANK, 6])
        mean_var = sb("mean_var", [P, 2, 2])
        group_mean = sb("group_mean", [P, 2])
        spread = sb("spread", [P, 2])
        eps = sb("eps", [P, 1])
        std = sb("std", [P, 2])
        rstd = sb("rstd", [P, 2])
        shift = sb("shift", [P, 2])

        consts_loaded = sem("consts_loaded")
        x_loaded = [sem(f"x_loaded{q}") for q in range(QUARTERS)]
        zeroed = sem("zeroed")
        stats_done = sem("stats_done")
        group_mm = sem("group_mm")
        small = sem("small")
        std_done = sem("std_done")
        xn_ready = sem("xn_ready")
        psum_full = sem("psum_full")
        psum_emptied = sem("psum_emptied")
        y_stored = [sem(f"y_stored{i}") for i in range(2)]
        pad_stored = sem("pad_stored")
        x_view = x.rearrange("b (k p) w c -> b p k (w c)", p=P)
        y_rows = y_dram.rearrange("b h w c -> b h (w c)")

        with nc.Block() as block:
            @block.sync
            def _(sp):
                sp.dma_start(dct_h[:], dct.rearrange("(k p) n -> p k n", p=P)).then_inc(consts_loaded, 16)
                sp.dma_start(avg[:], group_avg).then_inc(consts_loaded, 16)
                sp.wait_ge(zeroed, 1)
                for b in range(B):
                    for row in (0, H + 1):
                        sp.dma_start(y_rows[b, row].rearrange("(p n) -> p n", p=P), zero_row[:]
                                     ).then_inc(pad_stored, 16)
                with sp.Fori(0, B) as b:
                    with sp.Fori(0, QUARTERS) as q:
                        for slot in range(2):
                            sp.wait_ge(psum_emptied,
                                         F_BANKS + (b * QUARTERS + q) * F_TILES + 2 * (slot + 1) * BATCH)
                            sp.wait_ge(zeroed, 1)
                            for k in range(2):
                                sp.dma_start(y_rows[b, 1 + k * P:1 + (k + 1) * P,
                                                      bass.ds(q * QCOLS + slot * BATCH * BANK, BATCH * BANK)],
                                               y_sb[:, slot, k, :]).then_inc(y_stored[slot], 16)
                for slot in range(2):
                    sp.wait_ge(y_stored[slot], B * QUARTERS * 32 + 1)
                sp.wait_ge(pad_stored, 2 * B * 16)

            @block.gpsimd
            def _(pool):
                with pool.Fori(0, B) as b:
                    for q in range(QUARTERS):
                        pool.wait_ge(xn_ready, b * 2 * QUARTERS * TILES + (q + 1) * 2 * TILES)
                        pool.dma_start(x_sb[:, :, q * QCOLS:(q + 1) * QCOLS],
                                     x_view[b, :, :, q * QCOLS:(q + 1) * QCOLS]).then_inc(x_loaded[q], 16)

            @block.vector
            def _(dve):
                nc.vector.memset(zero_row[:], 0.0).then_inc(zeroed, 1)
                nc.vector.memset(eps[:], 1e-5).then_inc(zeroed, 1)
                nc.vector.memset(xn[:, 0, 0, 0:2], 0.0).then_inc(xn_ready, F_CREDIT)
                nc.vector.memset(xn[:, 1, 0, 0:2], 0.0).then_inc(psum_full, 8)
                nc.vector.memset(xn[:, 2, 0, 0:2], 0.0).then_inc(psum_emptied, F_BANKS)
                for slot in range(2):
                    nc.vector.memset(y_sb[:, slot, 0, 0:2], 0.0).then_inc(y_stored[slot], 1)
                with dve.Fori(0, B) as b:
                    for q in range(QUARTERS):
                        dve.wait_ge(x_loaded[q], b * 16 + 16)
                        for k in range(2):
                            for t in range(q * TILES, (q + 1) * TILES):
                                last = nc.vector.bn_stats(stats[:, k, t, :], x_sb[:, k, t * BANK:(t + 1) * BANK])
                    last.then_inc(stats_done, 1)
                    dve.wait_ge(stats_done, 2 * b + 1)
                    nc.vector.memset(spread[:], 0.0)
                    for k in range(2):
                        last = nc.vector.bn_aggr(mean_var[:, k, :], stats[:, k, :, :])
                    last.then_inc(stats_done, 1)
                    dve.wait_ge(group_mm, 2 * b + 1)
                    nc.vector.tensor_copy(group_mean[:], psum[:, 6, 0:2]).then_inc(small, 1)
                    dve.wait_ge(small, 7 * b + 1)
                    nc.vector.tensor_tensor(spread[:], mean_var[:, :, 0], group_mean[:], ALU.subtract
                                            ).then_inc(small, 1)
                    dve.wait_ge(small, 7 * b + 2)
                    nc.vector.tensor_tensor(spread[:], spread[:], spread[:], ALU.mult).then_inc(small, 1)
                    dve.wait_ge(small, 7 * b + 3)
                    nc.vector.tensor_tensor(spread[:], spread[:], mean_var[:, :, 1], ALU.add).then_inc(small, 1)
                    dve.wait_ge(std_done, b + 1)
                    nc.vector.reciprocal(rstd[:], std[:]).then_inc(small, 1)
                    dve.wait_ge(small, 7 * b + 5)
                    nc.vector.tensor_tensor(shift[:], group_mean[:], rstd[:], ALU.mult).then_inc(small, 1)
                    dve.wait_ge(small, 7 * b + 6)
                    nc.vector.tensor_scalar(shift[:], shift[:], -1.0, None, ALU.mult).then_inc(small, 1)
                    with dve.Fori(0, QUARTERS) as q:
                        for slot in range(2):
                            dve.wait_ge(y_stored[slot], (b * QUARTERS + q) * 32 + 1)
                            for j in range(BATCH):
                                for k in range(2):
                                    n = 2 * (slot * BATCH + j) + k
                                    bank = n % F_BANKS
                                    dve.wait_ge(psum_full, 8 + (b * QUARTERS + q) * F_TILES + n + 1)
                                    nc.vector.tensor_copy(y_sb[:, slot, k, j * BANK:(j + 1) * BANK],
                                                          psum[:, bank, :]).then_inc(psum_emptied, 1)

            @block.scalar
            def _(act):
                act.wait_ge(zeroed, 2)
                with act.Fori(0, B) as b:
                    act.wait_ge(group_mm, 2 * b + 2)
                    nc.scalar.activation(std[:], psum[:, 7, 0:2], ACT.Sqrt, bias=eps[:, 0:1]).then_inc(std_done, 1)
                    act.wait_ge(small, 7 * b + 7)
                    with act.Fori(0, QUARTERS) as q:
                        for t in range(TILES):
                            act.wait_ge(psum_full, (b * QUARTERS + q) * F_TILES + 2 * t + 2)
                            for k in range(2):
                                nc.scalar.activation(
                                    xn[:, t % 4, k, :], x_sb[:, k, bass.ds(q * QCOLS + t * BANK, BANK)],
                                    ACT.Identity, bias=shift[:, k:k + 1], scale=rstd[:, k:k + 1]
                                    ).then_inc(xn_ready, 1)

            @block.tensor
            def _(pe):
                pe.wait_ge(consts_loaded, 32)
                with pe.Fori(0, B) as b:
                    pe.wait_ge(stats_done, 2 * b + 2)
                    nc.tensor.matmul(psum[:, 6, 0:2], avg[:], mean_var[:, :, 0], start=True, stop=True
                                     ).then_inc(group_mm, 1)
                    pe.wait_ge(small, 7 * b + 4)
                    nc.tensor.matmul(psum[:, 7, 0:2], avg[:], spread[:], start=True, stop=True).then_inc(group_mm, 1)
                    with pe.Fori(0, QUARTERS) as q:
                        for t in range(TILES):
                            pe.wait_ge(xn_ready, F_CREDIT + (b * QUARTERS + q) * 2 * TILES + 2 * t + 2)
                            for m in range(2):
                                n = 2 * t + m
                                pe.wait_ge(psum_emptied, (b * QUARTERS + q) * F_TILES + n + 1)
                                for k in range(2):
                                    last = nc.tensor.matmul(psum[:, n % F_BANKS, :], dct_h[:, k, m * P:(m + 1) * P],
                                                            xn[:, t % 4, k, :], start=(k == 0), stop=(k == 1))
                                last.then_inc(psum_full, 1)


def mix_phase(nc, y_dram, z_dram, w, psum):
    with ExitStack() as ctx:
        def sb(name, shape):
            return ctx.enter_context(nc.sbuf_tensor("m_" + name, shape, F32))

        def sem(name):
            return ctx.enter_context(nc.semaphore("m_" + name))

        dct_w = sb("dct_w", [P, 2, W])
        idct_w = sb("idct_w", [P, 2, W])
        ident = sb("ident", [P, P])
        block_ones = sb("block_ones", [P, 2])
        ones32 = sb("ones32", [P, P])
        eye32 = sb("eye32", [P, 32])
        head_mask = sb("head_mask", [P, 32])
        minus_half = sb("minus_half", [P, 64])
        one = sb("one", [P, 1])
        wts = sb("wts", [P, 6, P])
        tap_w = sb("tap_w", [P, TAPS])
        taps = sb("taps", [P, TAPS, P])
        bias = sb("bias", [P, 1])
        rescale = sb("rescale", [P, 1])
        coef = sb("coef", [P, K, W])
        one_minus = sb("one_minus", [P, K, W])
        y_st = sb("y_st", [P, 2, ROWS, 2, C])
        xd = sb("xd", [P, NB, K * K])
        xh = sb("xh", [P, 2, W])
        h1 = sb("h1", [P, ROWS, W + 2])
        xc = sb("xc", [P, K, W])
        hi = sb("hi", [P, K, W])
        qk = sb("qk", [P, T2, 2, P])
        sq = sb("sq", [P, T2, 2, P])
        norm2 = sb("norm2", [P, 2, 2 * T2])
        rnorm = sb("rnorm", [P, 2, 2 * T2])
        rq = sb("rq", [P, 2 * T2])
        diag_rk = sb("diag_rk", [P, 2 * T2, 32])
        logits = sb("logits", [P, 2 * T2, 32])
        row_max = sb("row_max", [P, 2 * T2])
        row_sum = sb("row_sum", [P, 2 * T2])
        row_inv = sb("row_inv", [P, 2 * T2])
        attn = sb("attn", [P, 2 * T2, P])
        ap = sb("ap", [P, 2 * T2, P])
        v = sb("v", [P, NB, K * K])
        z = sb("z", [P, K, W])
        zt = sb("zt", [P, 2, K, P])
        out = sb("out", [P, 2, 2, K, C])

        consts_loaded = sem("consts_loaded")
        zeroed = sem("zeroed")
        weights_loaded = sem("weights_loaded")
        taps_ready = sem("taps_ready")
        y_loaded = sem("y_loaded")
        coef_loaded = sem("coef_loaded")
        one_minus_ready = sem("one_minus_ready")
        act_full = sem("act_full")
        act_emptied = sem("act_emptied")
        dve_full = sem("dve_full")
        dve_emptied = sem("dve_emptied")
        squared = sem("squared")
        pow_done = sem("pow_done")
        rq_ready = sem("rq_ready")
        diag_ready = sem("diag_ready")
        masked = sem("masked")
        max_ready = sem("max_ready")
        shifted = sem("shifted")
        exp_ready = sem("exp_ready")
        sum_ready = sem("sum_ready")
        inv_ready = sem("inv_ready")
        attn_ready = sem("attn_ready")
        xc_ready = sem("xc_ready")
        high_step = sem("high_step")
        z_ready = sem("z_ready")
        z_stored = sem("z_stored")

        act_idx = {name: i for i, name in enumerate(ACT_ORDER)}
        dve_idx = {name: i for i, name in enumerate(DVE_ORDER)}

        def act_bank(*name):
            return psum[:, act_idx[name] % ACT_BANKS, :]

        def dve_bank(*name):
            return psum[:, ACT_BANKS + dve_idx[name] % DVE_BANKS, :]

        def filled(order_idx, n_tiles, it, name):
            credit = ACT_CREDIT if order_idx is act_idx else 0
            return it * n_tiles + credit + order_idx[name] + 1

        def act_has(it, *name):
            return it * ACT_TILES + ACT_BANKS + act_idx[name] + 1

        def dve_has(it, *name):
            return it * DVE_TILES + DVE_BANKS + dve_idx[name] + 1

        def rows_view(t, r0, n):
            return t[:].rearrange("p w (r k) -> p r w k", k=K)[:, r0:r0 + n]

        with nc.Block() as block:
            @block.sync
            def _(sp):
                for dst, src in ((dct_w, w["dct"]), (idct_w, w["idct"])):
                    sp.dma_start(dst[:], src.rearrange("(k p) n -> p k n", p=P)).then_inc(consts_loaded, 16)
                for dst, src in ((ident, w["ident"]), (block_ones, w["block_ones"]), (ones32, w["ones32"]),
                                 (eye32, w["eye32"]), (head_mask, w["head_mask"])):
                    sp.dma_start(dst[:], src).then_inc(consts_loaded, 16)
                sp.wait_ge(zeroed, 1)
                for half in range(2):
                    r = slice(half * C, (half + 1) * C)
                    for i, name in enumerate(("c1a", "c2", "wv", "proj", "wq", "wk")):
                        sp.dma_start(wts[r, i, r], w[name]).then_inc(weights_loaded, 16)
                    sp.dma_start(tap_w[r, :], w["taps"]).then_inc(weights_loaded, 16)
                    sp.dma_start(bias[r, :], w["proj_b"].rearrange("(c n) -> c n", n=1)).then_inc(weights_loaded, 16)
                    for h in range(HEADS):
                        sp.dma_start(rescale[half * C + h * DH:half * C + (h + 1) * DH, :],
                                     w["rescale"][h:h + 1].partition_broadcast(DH)).then_inc(weights_loaded, 16)
                with sp.Fori(0, STRIPS) as s:
                    sp.wait_ge(dve_emptied, s * B * DVE_TILES + DVE_BANKS)
                    sp.wait_ge(zeroed, 1)
                    for half in range(2):
                        sp.dma_start(coef[half * C:(half + 1) * C],
                                     w["coef"][bass.ds(s * K + half * P, K), :].rearrange("r w -> (r w)")
                                     .partition_broadcast(C)).then_inc(coef_loaded, 16)
                    with sp.Fori(0, B) as b:
                        sp.wait_ge(act_full, (s * B + b) * ACT_TILES + 1)
                        sp.wait_ge(zeroed, 1)
                        for k in range(2):
                            for half in range(2):
                                sp.dma_start(y_st[:, k, :, half, :],
                                             y_dram[b, bass.ds(s * K + half * P, ROWS), k * P:(k + 1) * P, :]
                                             .rearrange("r w c -> w r c")).then_inc(y_loaded, 16)

            @block.gpsimd
            def _(pool):
                nc.gpsimd.memset(wts[:], 0.0).then_inc(zeroed, 1)
                nc.gpsimd.memset(attn[:], 0.0).then_inc(zeroed, 1)
                nc.gpsimd.memset(h1[:], 0.0).then_inc(zeroed, 1)
                nc.gpsimd.memset(minus_half[:], -0.5).then_inc(zeroed, 1)
                nc.gpsimd.memset(one[:], 1.0).then_inc(zeroed, 1)
                nc.gpsimd.memset(hi[:, 0, 0:1], 0.0).then_inc(high_step, 1)
                nc.gpsimd.memset(out[:, 0, 0, 0, 0:1], 0.0).then_inc(z_stored, 1)
                pool.wait_ge(consts_loaded, 7 * 16)
                pool.wait_ge(weights_loaded, 24 * 16)
                pool.wait_ge(zeroed, 5)
                with pool.Fori(0, STRIPS) as s:
                    pool.wait_ge(coef_loaded, s * 32 + 32)
                    nc.gpsimd.tensor_tensor(one_minus[:].rearrange("p r w -> p (r w)"),
                                            one[:].to_broadcast([P, K * W]), coef[:].rearrange("p r w -> p (r w)"),
                                            ALU.subtract).then_inc(one_minus_ready, 1)
                    with pool.Fori(0, B) as b:
                        it = pool.snap(s * B + b)
                        for j in range(8):
                            pool.wait_ge(dve_emptied, dve_has(it, "qk", j))
                            part = qk[:, 2 * j:2 * j + 2]
                            nc.gpsimd.tensor_tensor(sq[:, 2 * j:2 * j + 2], part, part, ALU.mult).then_inc(squared, 1)
                        pool.wait_ge(dve_emptied, dve_has(it, "norm", 0))
                        nc.gpsimd.tensor_tensor(rnorm[:].rearrange("p a b -> p (a b)"),
                                                norm2[:].rearrange("p a b -> p (a b)"), minus_half[:], ALU.pow
                                                ).then_inc(pow_done, 1)
                        pool.wait_ge(pow_done, it + 1)
                        nc.gpsimd.tensor_tensor(diag_rk[:], rnorm[:, 1, :].unsqueeze(2).to_broadcast([P, 2 * T2, 32]),
                                                eye32[:].unsqueeze(1).to_broadcast([P, 2 * T2, 32]), ALU.mult
                                                ).then_inc(diag_ready, 1)
                        nc.gpsimd.tensor_scalar(rq[:], rnorm[:, 0, :], rescale[:, 0:1], None, ALU.mult
                                                ).then_inc(rq_ready, 1)

                        def x_conv(i):
                            pool.wait_ge(act_emptied, act_has(it, "conv", i))
                            part = xc[:, 2 * i:2 * i + 2, :].rearrange("p r (w k) -> p r w k", k=K)
                            nc.gpsimd.tensor_tensor(part, part, rows_view(xd, 2 * i, 2), ALU.add
                                                    ).then_inc(xc_ready, 1)

                        def x_high(i):
                            rows = slice(2 * i, 2 * i + 2)
                            pool.wait_ge(act_emptied, act_has(it, "c2", i))
                            nc.gpsimd.tensor_tensor(hi[:, rows], hi[:, rows], xc[:, rows], ALU.add
                                                    ).then_inc(high_step, 1)
                            pool.wait_ge(high_step, it * 12 + 3 * i + 2)
                            nc.gpsimd.tensor_tensor(hi[:, rows], hi[:, rows], one_minus[:, rows], ALU.mult
                                                    ).then_inc(high_step, 1)
                            pool.wait_ge(high_step, it * 12 + 3 * i + 3)
                            part = hi[:, rows, :].rearrange("p r (w k) -> p r w k", k=K)
                            nc.gpsimd.tensor_tensor(part, part, rows_view(xd, 2 * i, 2), ALU.add
                                                    ).then_inc(high_step, 1)

                        x_conv(0)
                        x_conv(1)
                        pool.wait_ge(dve_emptied, dve_has(it, "rk", 1))
                        nc.gpsimd.tensor_tensor(logits[:], logits[:],
                                                head_mask[:].unsqueeze(1).to_broadcast([P, 2 * T2, 32]), ALU.add
                                                ).then_inc(masked, 1)
                        pool.wait_ge(max_ready, it + 1)
                        nc.gpsimd.tensor_tensor(logits[:], logits[:],
                                                row_max[:].unsqueeze(2).to_broadcast([P, 2 * T2, 32]), ALU.subtract
                                                ).then_inc(shifted, 1)
                        x_conv(2)
                        x_high(0)
                        x_conv(3)
                        x_high(1)
                        x_high(2)
                        x_high(3)

            @block.scalar
            def _(act):
                act.wait_ge(zeroed, 5)
                nc.scalar.activation(row_sum[:], minus_half[:, 0:2 * T2], ACT.Identity).then_inc(act_emptied, ACT_BANKS)
                nc.scalar.activation(row_inv[:], minus_half[:, 0:2 * T2], ACT.Identity).then_inc(act_full, ACT_CREDIT)
                z_view = z_dram.rearrange("b w (g r) c -> b w g (r c)", g=2)
                with act.Fori(0, STRIPS) as s, act.Fori(0, B) as b:
                    it = act.snap(s * B + b)
                    def empty(out_ap, in_ap, func, *name):
                        act.wait_ge(act_full, filled(act_idx, ACT_TILES, it, name))
                        nc.scalar.activation(out_ap, in_ap, func).then_inc(act_emptied, 1)

                    def two_rows(*name):
                        return act_bank(*name).rearrange("p (r w) -> p r w", r=2)

                    act.wait_ge(high_step, it * 12 + 1)
                    empty(xh[:], two_rows("dct", 0), ACT.Identity, "dct", 0)
                    for j in range(4):
                        empty(rows_view(xd, 2 * j, 2),
                              act_bank("dct", j + 1).rearrange("p (r w k) -> p r w k", r=2, k=K),
                              ACT.Identity, "dct", j + 1)
                    empty(h1[:, 0:ROWS:ROWS - 1, 1:W + 1], two_rows("c1", 0), ACT.Gelu, "c1", 0)
                    for j in range(4):
                        empty(h1[:, 2 * j + 1:2 * j + 3, 1:W + 1], two_rows("c1", j + 1), ACT.Gelu, "c1", j + 1)
                    for name in ACT_ORDER[10:]:
                        kind, j = name
                        if name == ("conv", 3):
                            act.wait_ge(shifted, it + 1)
                            nc.scalar.activation(logits[:], logits[:], ACT.Exp).then_inc(exp_ready, 1)
                        if kind == "conv":
                            empty(xc[:, 2 * j:2 * j + 2], two_rows(*name), ACT.Gelu, *name)
                        elif kind == "c2":
                            empty(hi[:, 2 * j:2 * j + 2], two_rows(*name), ACT.Gelu, *name)
                        elif kind == "v":
                            empty(v[:, 8 * j:8 * j + 8].rearrange("p w k -> p (w k)"), act_bank(*name),
                                  ACT.Identity, *name)
                        else:
                            empty(ap[:, 4 * j:4 * j + 4].rearrange("p w k -> p (w k)"), act_bank(*name),
                                  ACT.Identity, *name)
                    act.wait_ge(dve_emptied, dve_has(it, "idct", 3))
                    for k in range(2):
                        act.dma_start(z_view[b, k * P:(k + 1) * P, :, bass.ds(s * K * C, K * C)],
                                      out[:, k].rearrange("p g r c -> p g (r c)")).then_inc(z_stored, 16)
                act.wait_ge(z_stored, STRIPS * B * 32 + 1)

            @block.vector
            def _(dve):
                dve.wait_ge(consts_loaded, 7 * 16)
                dve.wait_ge(weights_loaded, 24 * 16)
                for t in range(TAPS):
                    nc.vector.tensor_scalar(taps[:, t, :], ident[:], tap_w[:, t:t + 1], None, ALU.mult
                                            ).then_inc(taps_ready, 1)
                nc.vector.memset(row_max[:], 0.0).then_inc(dve_emptied, DVE_BANKS)
                with dve.Fori(0, STRIPS * B) as it:
                    def full(*name):
                        dve.wait_ge(dve_full, filled(dve_idx, DVE_TILES, it, name))

                    for j in range(8):
                        full("qk", j)
                        nc.vector.tensor_copy(qk[:, 2 * j:2 * j + 2].rearrange("p a b c -> p (a b c)"),
                                              dve_bank("qk", j)).then_inc(dve_emptied, 1)
                    full("norm", 0)
                    nc.vector.tensor_scalar(norm2[:].rearrange("p a b -> p (a b)"), dve_bank("norm", 0)[:, 0:64],
                                            1e-24, None, ALU.max).then_inc(dve_emptied, 1)
                    dve.wait_ge(rq_ready, it + 1)
                    for j in range(2):
                        blocks = slice(j * T2, (j + 1) * T2)
                        full("s", j)
                        nc.vector.tensor_tensor(logits[:, blocks],
                                                dve_bank("s", j).rearrange("p (t e) -> p t e", e=32),
                                                rq[:, blocks].unsqueeze(2).to_broadcast([P, T2, 32]), ALU.mult
                                                ).then_inc(dve_emptied, 1)
                    for j in range(2):
                        blocks = slice(j * T2, (j + 1) * T2)
                        full("rk", j)
                        dve.wait_ge(dve_emptied, dve_has(it, "s", j))
                        nc.vector.tensor_tensor(logits[:, blocks],
                                                dve_bank("rk", j).rearrange("p (t e) -> p t e", e=32),
                                                logits[:, blocks], ALU.mult).then_inc(dve_emptied, 1)
                    dve.wait_ge(masked, it + 1)
                    nc.vector.tensor_reduce(row_max[:], logits[:], AX.X, ALU.max).then_inc(max_ready, 1)
                    dve.wait_ge(exp_ready, it + 1)
                    nc.vector.tensor_reduce(row_sum[:], logits[:], AX.X, ALU.add).then_inc(sum_ready, 1)
                    dve.wait_ge(sum_ready, it + 1)
                    nc.vector.reciprocal(row_inv[:], row_sum[:]).then_inc(inv_ready, 1)
                    dve.wait_ge(inv_ready, it + 1)
                    for j in range(4):
                        r = slice(32 * j, 32 * j + 32)
                        nc.vector.tensor_tensor(attn[r, :, r], logits[r],
                                                row_inv[r].unsqueeze(2).to_broadcast([32, 2 * T2, 32]), ALU.mult
                                                ).then_inc(attn_ready, 1)
                    for q in range(4):
                        part = slice(64 * q, 64 * q + 64)
                        full("low", q)
                        nc.vector.scalar_tensor_tensor(out=z[:, :, part],
                                                       in0=dve_bank("low", q).rearrange("p (r w) -> p r w", r=K),
                                                       scalar=bias[:, 0:1], in1=coef[:, :, part],
                                                       op0=ALU.add, op1=ALU.mult).then_inc(dve_emptied, 1)
                        dve.wait_ge(dve_emptied, dve_has(it, "low", q))
                        dve.wait_ge(high_step, it * 12 + 13)
                        nc.vector.tensor_tensor(z[:, :, part], z[:, :, part], hi[:, :, part], ALU.add
                                                ).then_inc(z_ready, 1)
                    for j in range(4):
                        full("t", j)
                        nc.vector.tensor_copy(zt[:, j // 2, 4 * (j % 2):4 * (j % 2) + 4].rearrange("p r c -> p (r c)"),
                                              dve_bank("t", j)).then_inc(dve_emptied, 1)
                    dve.wait_ge(z_stored, it * 32 + 1)
                    for j in range(4):
                        full("idct", j)
                        rows = slice(4 * (j % 2), 4 * (j % 2) + 4)
                        nc.vector.tensor_copy(out[:, j // 2, :, rows, :].rearrange("p g r c -> p r g c"),
                                              dve_bank("idct", j).rearrange("p (r g c) -> p r g c", r=4, g=2)
                                              ).then_inc(dve_emptied, 1)

            @block.tensor
            def _(pe):
                pe.wait_ge(consts_loaded, 7 * 16)
                pe.wait_ge(weights_loaded, 24 * 16)
                pe.wait_ge(taps_ready, TAPS)
                pe.wait_ge(zeroed, 5)
                c1a_w, c2_w, v_w, proj_w = (wts[:, i, :] for i in range(4))
                qk_w = wts[:, 4:6, :].rearrange("p a b -> p (a b)")
                with pe.Fori(0, STRIPS * B) as it:
                    def act_tile(*name):
                        pe.wait_ge(act_emptied, it * ACT_TILES + act_idx[name] + 1)
                        return act_bank(*name)

                    def dve_tile(*name):
                        pe.wait_ge(dve_emptied, it * DVE_TILES + dve_idx[name] + 1)
                        return dve_bank(*name)

                    def conv(i):
                        pe.wait_ge(act_emptied, act_has(it, "c1", 4))
                        bank = act_tile("conv", i)
                        for t in range(TAPS):
                            dr, dw = t // 3, t % 3
                            last = nc.tensor.matmul(bank, taps[:, t, :], h1[:, 2 * i + dr:2 * i + dr + 2, dw:dw + W],
                                                    start=(t == 0), stop=(t == TAPS - 1))
                        last.then_inc(act_full, 1)

                    def c2(i):
                        pe.wait_ge(xc_ready, it * 4 + i + 1)
                        nc.tensor.matmul(act_tile("c2", i), c2_w, xc[:, 2 * i:2 * i + 2, :],
                                         start=True, stop=True).then_inc(act_full, 1)

                    pe.wait_ge(y_loaded, it * 64 + 64)
                    for j in range(5):
                        bank = act_tile("dct", j)
                        for n, row in enumerate((0, ROWS - 1) if j == 0 else (2 * j - 1, 2 * j)):
                            for k in range(2):
                                last = nc.tensor.matmul(bank[:, n * W:(n + 1) * W],
                                                        y_st[:, k, row].rearrange("p g c -> p (g c)"), dct_w[:, k, :],
                                                        start=(k == 0), stop=(k == 1))
                        last.then_inc(act_full, 1)
                    for j in range(5):
                        pe.wait_ge(act_emptied, act_has(it, "dct", j))
                        nc.tensor.matmul(act_tile("c1", j), c1a_w, xh[:] if j == 0 else rows_view(xd, 2 * j - 2, 2),
                                         start=True, stop=True).then_inc(act_full, 1)
                    for j in range(8):
                        bank = dve_tile("qk", j)
                        for t in range(2):
                            pair = 2 * j + t
                            last = nc.tensor.matmul(bank[:, t * 256:(t + 1) * 256],
                                                    xd[:, 2 * pair:2 * pair + 2].rearrange("p w k -> p (w k)"), qk_w,
                                                    start=True, stop=True)
                        last.then_inc(dve_full, 1)
                    conv(0)
                    bank = dve_tile("norm", 0)[:, 0:64].rearrange("p (q b t) -> p q b t", q=2, b=2)
                    for t in range(T2):
                        if t % 2 == 0:
                            pe.wait_ge(squared, it * 8 + t // 2 + 1)
                        for q in range(2):
                            last = nc.tensor.matmul(bank[:, q, :, t], sq[:, t, q, :], block_ones[:],
                                                    start=True, stop=True)
                    last.then_inc(dve_full, 1)
                    s_banks = [dve_tile("s", b) for b in range(2)]
                    pe.wait_ge(dve_emptied, dve_has(it, "qk", 7))
                    conv(1)
                    for b in range(2):
                        bank = s_banks[b]
                        pos = slice(64 * b, 64 * b + 64)
                        for t in range(T2):
                            for g in range(4):
                                ch = slice(32 * g, 32 * g + 32)
                                last = nc.tensor.matmul(bank[ch, 32 * t:32 * t + 32], qk[pos, t, 0, ch],
                                                        qk[pos, t, 1, ch], start=True, stop=True)
                        last.then_inc(dve_full, 1)
                    pe.wait_ge(diag_ready, it + 1)
                    for b in range(2):
                        nc.tensor.matmul(dve_tile("rk", b), ones32[:],
                                         diag_rk[:, b * T2:(b + 1) * T2].rearrange("p t e -> p (t e)"),
                                         start=True, stop=True).then_inc(dve_full, 1)
                    conv(2)
                    c2(0)
                    conv(3)
                    c2(1)
                    for j in range(4):
                        nc.tensor.matmul(act_tile("v", j), v_w, xd[:, 8 * j:8 * j + 8].rearrange("p w k -> p (w k)"),
                                         start=True, stop=True).then_inc(act_full, 1)
                    c2(2)
                    c2(3)
                    pe.wait_ge(attn_ready, it * 4 + 4)
                    for j in range(8):
                        bank = act_tile("u", j)
                        for n in range(4):
                            last = nc.tensor.matmul(bank[:, n * P:(n + 1) * P], attn[:, 4 * j + n, :], proj_w,
                                                    start=True, stop=True)
                        last.then_inc(act_full, 1)
                    pe.wait_ge(act_emptied, act_has(it, "u", 7))
                    for q in range(4):
                        bank = dve_tile("low", q).rearrange("p (r w) -> p r w", r=K)
                        for n in range(8):
                            wb = 8 * q + n
                            last = nc.tensor.matmul(bank[:, :, n * K:(n + 1) * K], ap[:, (wb % 2) * T2 + wb // 2, :],
                                                    v[:, wb, :], start=True, stop=True)
                        last.then_inc(dve_full, 1)
                    for j in range(4):
                        pe.wait_ge(z_ready, it * 4 + 2 * (j // 2) + 2)
                        bank = dve_tile("t", j)
                        for r in range(4):
                            last = nc.tensor.transpose(bank[:, r * P:(r + 1) * P],
                                                       z[:, 4 * (j % 2) + r, (j // 2) * P:(j // 2 + 1) * P], ident[:])
                        last.then_inc(dve_full, 1)
                    for j in range(4):
                        rows = slice(4 * (j % 2), 4 * (j % 2) + 4)
                        pe.wait_ge(dve_emptied, dve_has(it, "t", 2 + j % 2))
                        bank = dve_tile("idct", j)
                        for k in range(2):
                            last = nc.tensor.matmul(bank, idct_w[:, k, (j // 2) * P:(j // 2 + 1) * P],
                                                    zt[:, k, rows].rearrange("p r c -> p (r c)"),
                                                    start=(k == 0), stop=(k == 1))
                        last.then_inc(dve_full, 1)


def inverse_phase(nc, x, z_dram, idct, out, psum):
    with ExitStack() as ctx:
        def sb(name, shape):
            return ctx.enter_context(nc.sbuf_tensor("i_" + name, shape, F32))

        def sem(name):
            return ctx.enter_context(nc.semaphore("i_" + name))

        idct_h = sb("idct_h", [P, 2, H])
        z_sb = sb("z_sb", [P, 2, 2, WT * C])
        x_sb = sb("x_sb", [P, 2, 2, WT * C])
        o_sb = sb("o_sb", [P, 2, 2, WT * C])

        consts_loaded = sem("consts_loaded")
        z_loaded = [sem(f"z_loaded{i}") for i in range(2)]
        x_loaded = [sem(f"x_loaded{i}") for i in range(2)]
        z_used = sem("z_used")
        psum_full = sem("psum_full")
        psum_emptied = sem("psum_emptied")
        stored = [sem(f"stored{i}") for i in range(2)]
        x_view = x.rearrange("b (k p) w c -> b p k (w c)", p=P)
        out_view = out.rearrange("b (k p) w c -> b p k (w c)", p=P)

        with nc.Block() as block:
            @block.sync
            def _(sp):
                sp.dma_start(idct_h[:], idct.rearrange("(k p) n -> p k n", p=P)).then_inc(consts_loaded, 16)
                with sp.Fori(0, B) as b:
                    with sp.Fori(0, I_STEPS) as i:
                        for slot in range(2):
                            sp.wait_ge(psum_emptied, (b * I_STEPS + i) * 8 + 4 * slot + 4)
                            for k in range(2):
                                sp.dma_start(z_sb[:, slot, k].rearrange("p (w c) -> p w c", c=C),
                                             z_dram[b, bass.ds(i * 2 * WT + slot * WT, WT), k * P:(k + 1) * P, :]
                                             .rearrange("w k c -> k w c")).then_inc(z_loaded[slot], 16)
                            sp.dma_start(x_sb[:, slot], x_view[b, :, :, bass.ds((i * 2 + slot) * WT * C, WT * C)]
                                         ).then_inc(x_loaded[slot], 16)

            @block.tensor
            def _(pe):
                pe.wait_ge(consts_loaded, 16)
                with pe.Fori(0, B * I_STEPS) as it:
                    for slot in range(2):
                        pe.wait_ge(z_loaded[slot], it * 32 + 32)
                        for m in range(2):
                            for c in range(2):
                                n = 4 * slot + 2 * m + c
                                pe.wait_ge(psum_emptied, it * 8 + n + 1)
                                for k in range(2):
                                    last = nc.tensor.matmul(psum[:, n, :], idct_h[:, k, m * P:(m + 1) * P],
                                                            z_sb[:, slot, k, c * BANK:(c + 1) * BANK],
                                                            start=(k == 0), stop=(k == 1))
                                last.then_inc(psum_full, 1)

            @block.vector
            def _(dve):
                nc.vector.memset(o_sb[:, 0, 0, 0:2], 0.0).then_inc(psum_emptied, 8)
                for slot in range(2):
                    nc.vector.memset(o_sb[:, slot, 1, 0:2], 0.0).then_inc(stored[slot], 1)
                with dve.Fori(0, B * I_STEPS) as it:
                    for slot in range(2):
                        dve.wait_ge(x_loaded[slot], it * 16 + 16)
                        dve.wait_ge(stored[slot], it * 16 + 1)
                        for m in range(2):
                            for c in range(2):
                                n = 4 * slot + 2 * m + c
                                dve.wait_ge(psum_full, it * 8 + n + 1)
                                cols = slice(c * BANK, (c + 1) * BANK)
                                nc.vector.tensor_tensor(o_sb[:, slot, m, cols], psum[:, n, :], x_sb[:, slot, m, cols],
                                                        ALU.add).then_inc(psum_emptied, 1)

            @block.scalar
            def _(act):
                with act.Fori(0, B) as b:
                    with act.Fori(0, I_STEPS) as i:
                        for slot in range(2):
                            act.wait_ge(psum_emptied, (b * I_STEPS + i) * 8 + 4 * slot + 12)
                            act.dma_start(out_view[b, :, :, bass.ds((i * 2 + slot) * WT * C, WT * C)],
                                          o_sb[:, slot]).then_inc(stored[slot], 16)
                for slot in range(2):
                    act.wait_ge(stored[slot], B * I_STEPS * 16 + 1)


def build(nc, args, out):
    y_dram = nc.dram_tensor("y_dram", (B, H + 2, W, C), F32, kind="Internal").ap()
    z_dram = nc.dram_tensor("z_dram", (B, W, H, C), F32, kind="Internal").ap()
    with nc.psum_tensor("psum", [P, 8, BANK], F32) as psum:
        forward_phase(nc, args["x"], y_dram, args["dct"], args["group_avg"], psum)
        mix_phase(nc, y_dram, z_dram, args, psum)
        inverse_phase(nc, args["x"], z_dram, args["idct"], out, psum)


def shape_constants():
    import numpy as np

    n = np.arange(H)
    cos = np.cos(np.pi * (2 * n[None, :] + 1) * n[:, None] / (2 * H))
    wk = np.ones(H)
    wk[0] = 0.5
    p = np.arange(P)
    return {
        "dct": np.ascontiguousarray((2.0 * cos).T).astype(np.float32),
        "idct": (wk[:, None] * cos / H).astype(np.float32),
        "group_avg": ((p[:, None] // GROUP_ROWS == p[None, :] // GROUP_ROWS) / GROUP_ROWS).astype(np.float32),
        "ident": np.eye(P, dtype=np.float32),
        "block_ones": (p[:, None] // C == np.arange(2)[None, :]).astype(np.float32),
        "ones32": (p[:, None] // 32 == p[None, :] // 32).astype(np.float32),
        "eye32": (p[:, None] % 32 == np.arange(32)[None, :]).astype(np.float32),
        "head_mask": np.where(p[:, None] % 32 // DH == np.arange(32)[None, :] // DH, 0, -1e30).astype(np.float32),
    }


def kernel(x, L0_conv_Wq, L0_conv_Wk, L0_conv_Wv, L0_conv_rescale, L0_conv_proj_w, L0_conv_proj_b,
           L0_conv_c1a_w, L0_conv_c1b_w, L0_conv_c2_w, L0_conv_coef_emb):
    import numpy as np
    import concourse.bacc as bacc
    from concourse.bass_utils import run_bass_kernel_spmd

    arrays = {
        "x": x, "wq": L0_conv_Wq, "wk": L0_conv_Wk, "wv": L0_conv_Wv, "proj": L0_conv_proj_w,
        "proj_b": L0_conv_proj_b, "rescale": np.asarray(L0_conv_rescale).reshape(HEADS, 1),
        "c1a": np.asarray(L0_conv_c1a_w).reshape(C, C).T, "c2": np.asarray(L0_conv_c2_w).reshape(C, C).T,
        "taps": np.asarray(L0_conv_c1b_w).reshape(C, TAPS), "coef": L0_conv_coef_emb,
        **shape_constants(),
    }
    arrays = {name: np.ascontiguousarray(a) for name, a in arrays.items()}
    nc = bacc.Bacc("TRN2", target_bir_lowering=False, num_devices=1)
    args = {name: nc.dram_tensor(name, a.shape, mybir.dt.from_np(a.dtype), kind="ExternalInput").ap()
            for name, a in arrays.items()}
    out = nc.dram_tensor("result", (B, H, W, C), F32, kind="ExternalOutput").ap()
    build(nc, args, out)
    return run_bass_kernel_spmd(nc, [arrays], core_ids=[0]).results[0]["result"]
```

```python
from contextlib import ExitStack

import concourse.bass as bass
from concourse import mybir

F32 = mybir.dt.float32
ALU = mybir.AluOpType
ACT = mybir.ActivationFunctionType
AX = mybir.AxisListType

P = 128
B, H, W, C = 4, 256, 256, 64
GROUP_ROWS = 8
K = 8
HEADS, DH = 4, 16
BANK = 512

HW = W // 2
COLS = HW * C
QUARTERS = 4
QCOLS = COLS // QUARTERS
TILES = QCOLS // BANK
BATCH = 2
F_TILES = 2 * TILES
XN_CREDIT = 4 * TILES * QUARTERS
LEFT_BANKS, RIGHT_BANKS = 2, 4

STRIPS = H // 2 // K
ROWS = K + 2
NB = W // K
T2 = NB // 2
TAPS = 9
PE_TAPS = 2
DVE_TAPS = TAPS - PE_TAPS
ACT_ORDER = ([("c2", 3)] + [("dct", j) for j in range(5)] + [("c1", j) for j in range(5)] + [("qk", j) for j in range(8)]
             + [("v", j) for j in range(4)] + [("t", j) for j in range(4)] + [("idct", j) for j in range(4)]
             + [("c2", j) for j in range(3)] + [("u", j) for j in range(4)] + [("none", 0)])
DVE_ORDER = ([("norm", 0), ("s", 0), ("rk", 0), ("s", 1), ("rk", 1)] + [("low", j) for j in range(4)])
U_BLOCKS = (0, 2, 1, 3)
ACT_TILES, DVE_TILES = len(ACT_ORDER), len(DVE_ORDER)
ACT_BANKS, DVE_BANKS, CONV_BANKS = 3, 3, 2
ACT_IDX = {name: i for i, name in enumerate(ACT_ORDER)}
DVE_IDX = {name: i for i, name in enumerate(DVE_ORDER)}
LAST = STRIPS * B
ACT_CREDIT = ACT_TILES - 5
assert ACT_TILES % ACT_BANKS == 0 and DVE_TILES % DVE_BANKS == 0

WT = 8
I_STEPS = HW // WT // 2


def forward_phase(nc, x, y_dram, dct, group_avg, psum):
    with ExitStack() as ctx:
        def sb(name, shape):
            return ctx.enter_context(nc.sbuf_tensor("f_" + name, shape, F32))

        def sem(name):
            return ctx.enter_context(nc.semaphore("f_" + name))

        x_sb = sb("x_sb", [P, 2, 2, COLS])
        xn = sb("xn", [P, 2, 2, 2, BANK])
        left = sb("left", [P, 4, BANK])
        y_sb = sb("y_sb", [P, 2, 2, 2, BATCH * BANK])
        dct_h = sb("dct_h", [P, 2, H])
        avg = sb("avg", [P, P])
        zero_row = sb("zero_row", [P, W * C // P])
        stats = sb("stats", [P, 2, 2 * COLS // BANK, 6])
        mean_var = sb("mean_var", [P, 2, 2])
        group_mean = sb("group_mean", [P, 2])
        spread = sb("spread", [P, 2])
        eps = sb("eps", [P, 1])
        std = sb("std", [P, 2])
        rstd = sb("rstd", [P, 2])
        shift = sb("shift", [P, 2])

        consts_loaded = sem("consts_loaded")
        x_loaded = [sem(f"x_loaded{q}") for q in range(QUARTERS)]
        zeroed = sem("zeroed")
        stats_done = sem("stats_done")
        group_mm = sem("group_mm")
        small = sem("small")
        std_done = sem("std_done")
        xn_ready = sem("xn_ready")
        left_full = sem("left_full")
        left_ready = sem("left_ready")
        right_full = sem("right_full")
        right_used = sem("right_used")
        y_stored = [sem(f"y_stored{i}") for i in range(2)]
        pad_stored = sem("pad_stored")
        x_view = x.rearrange("b (k p) g w c -> b p k g (w c)", p=P)
        y_rows = y_dram.rearrange("b h g w c -> b h g (w c)")

        with nc.Block() as block:
            @block.sync
            def _(sp):
                sp.dma_start(dct_h[:], dct.rearrange("(k p) n -> p k n", p=P)).then_inc(consts_loaded, 16)
                sp.dma_start(avg[:], group_avg).then_inc(consts_loaded, 16)
                sp.wait_ge(zeroed, 1)
                for b in range(B):
                    for row in (0, H + 1):
                        sp.dma_start(y_rows[b, row].rearrange("g (p n) -> (g p) n", p=P // 2), zero_row[:]
                                     ).then_inc(pad_stored, 16)
                with sp.Fori(0, B) as b:
                    with sp.Fori(0, QUARTERS) as q:
                        for slot in range(2):
                            sp.wait_ge(right_used, RIGHT_BANKS + (b * QUARTERS + q) * F_TILES + 2 * (slot + 1) * BATCH)
                            sp.wait_ge(zeroed, 1)
                            for m in range(2):
                                sp.dma_start(y_rows[b, 1 + m * P:1 + (m + 1) * P, :,
                                                    bass.ds(q * QCOLS + slot * BATCH * BANK, BATCH * BANK)],
                                             y_sb[:, slot, m]).then_inc(y_stored[slot], 16)
                sp.wait_ge(pad_stored, 2 * B * 16)
                for slot in range(2):
                    sp.wait_ge(y_stored[slot], B * QUARTERS * 32 + 1)

            @block.gpsimd
            def _(pool):
                with pool.Fori(0, B) as b:
                    for q in range(QUARTERS):
                        pool.wait_ge(xn_ready, b * XN_CREDIT + (q + 1) * 4 * TILES)
                        for k in range(2):
                            pool.dma_start(x_sb[:, k, :, q * QCOLS:(q + 1) * QCOLS],
                                           x_view[b, :, k, :, q * QCOLS:(q + 1) * QCOLS]).then_inc(x_loaded[q], 16)

            @block.vector
            def _(dve):
                nc.vector.memset(zero_row[:], 0.0).then_inc(zeroed, 1)
                nc.vector.memset(eps[:], 1e-5).then_inc(zeroed, 1)
                nc.vector.memset(xn[:, 0, 0, 0, 0:2], 0.0).then_inc(xn_ready, XN_CREDIT)
                nc.vector.memset(left[:, 0, 0:2], 0.0).then_inc(left_ready, LEFT_BANKS)
                nc.vector.memset(left[:, 1, 0:2], 0.0).then_inc(right_full, 4)
                nc.vector.memset(left[:, 2, 0:2], 0.0).then_inc(right_used, RIGHT_BANKS)
                for slot in range(2):
                    nc.vector.memset(y_sb[:, slot, 0, 0, 0:2], 0.0).then_inc(y_stored[slot], 1)
                with dve.Fori(0, B) as b:
                    for q in range(QUARTERS):
                        dve.wait_ge(x_loaded[q], b * 32 + 32)
                        for k in range(2):
                            for g in range(2):
                                for t in range(q * TILES, (q + 1) * TILES):
                                    last = nc.vector.bn_stats(stats[:, k, g * (COLS // BANK) + t, :],
                                                              x_sb[:, k, g, t * BANK:(t + 1) * BANK])
                    last.then_inc(stats_done, 1)
                    dve.wait_ge(stats_done, 2 * b + 1)
                    nc.vector.memset(spread[:], 0.0)
                    for k in range(2):
                        last = nc.vector.bn_aggr(mean_var[:, k, :], stats[:, k, :, :])
                    last.then_inc(stats_done, 1)
                    dve.wait_ge(group_mm, 2 * b + 1)
                    nc.vector.tensor_copy(group_mean[:], psum[:, 6, 0:2]).then_inc(small, 1)
                    dve.wait_ge(small, 7 * b + 1)
                    nc.vector.tensor_tensor(spread[:], mean_var[:, :, 0], group_mean[:], ALU.subtract
                                            ).then_inc(small, 1)
                    dve.wait_ge(small, 7 * b + 2)
                    nc.vector.tensor_tensor(spread[:], spread[:], spread[:], ALU.mult).then_inc(small, 1)
                    dve.wait_ge(small, 7 * b + 3)
                    nc.vector.tensor_tensor(spread[:], spread[:], mean_var[:, :, 1], ALU.add).then_inc(small, 1)
                    dve.wait_ge(std_done, b + 1)
                    nc.vector.reciprocal(rstd[:], std[:]).then_inc(small, 1)
                    dve.wait_ge(small, 7 * b + 5)
                    nc.vector.tensor_tensor(shift[:], group_mean[:], rstd[:], ALU.mult).then_inc(small, 1)
                    dve.wait_ge(small, 7 * b + 6)
                    nc.vector.tensor_scalar(shift[:], shift[:], -1.0, None, ALU.mult).then_inc(small, 1)
                    with dve.Fori(0, QUARTERS) as q:
                        for slot in range(2):
                            dve.wait_ge(y_stored[slot], (b * QUARTERS + q) * 32 + 1)
                            for j in range(BATCH):
                                for m in range(2):
                                    n = 2 * (slot * BATCH + j) + m
                                    count = (b * QUARTERS + q) * F_TILES + n + 1
                                    dve.wait_ge(right_full, 4 + count)
                                    dve.wait_ge(left_ready, LEFT_BANKS + count)
                                    cols = slice(j * BANK, (j + 1) * BANK)
                                    right = psum[:, LEFT_BANKS + n % RIGHT_BANKS, :]
                                    nc.vector.tensor_tensor(y_sb[:, slot, m, 0, cols], left[:, n % 4, :], right, ALU.add)
                                    nc.vector.tensor_tensor(y_sb[:, slot, m, 1, cols], left[:, n % 4, :], right,
                                                            ALU.subtract).then_inc(right_used, 1)

            @block.scalar
            def _(act):
                act.wait_ge(zeroed, 2)
                with act.Fori(0, B) as b:
                    act.wait_ge(group_mm, 2 * b + 2)
                    nc.scalar.activation(std[:], psum[:, 7, 0:2], ACT.Sqrt, bias=eps[:, 0:1]).then_inc(std_done, 1)
                    act.wait_ge(small, 7 * b + 7)
                    with act.Fori(0, QUARTERS) as q:
                        def normalise(t):
                            act.wait_ge(right_full, (b * QUARTERS + q) * F_TILES + 2 * t + 2)
                            for g in range(2):
                                for k in range(2):
                                    nc.scalar.activation(
                                        xn[:, t % 2, g, k, :], x_sb[:, k, g, bass.ds(q * QCOLS + t * BANK, BANK)],
                                        ACT.Identity, bias=shift[:, k:k + 1], scale=rstd[:, k:k + 1]
                                    ).then_inc(xn_ready, 1)

                        def keep_left(t):
                            for m in range(2):
                                n = 2 * t + m
                                act.wait_ge(left_full, (b * QUARTERS + q) * F_TILES + n + 1)
                                act.wait_ge(right_used, (b * QUARTERS + q) * F_TILES + n + 1)
                                nc.scalar.activation(left[:, n % 4, :], psum[:, n % LEFT_BANKS, :], ACT.Identity
                                                     ).then_inc(left_ready, 1)

                        normalise(0)
                        for t in range(1, TILES):
                            normalise(t)
                            keep_left(t - 1)
                        keep_left(TILES - 1)

            @block.tensor
            def _(pe):
                pe.wait_ge(consts_loaded, 32)
                with pe.Fori(0, B) as b:
                    pe.wait_ge(stats_done, 2 * b + 2)
                    nc.tensor.matmul(psum[:, 6, 0:2], avg[:], mean_var[:, :, 0], start=True, stop=True
                                     ).then_inc(group_mm, 1)
                    pe.wait_ge(small, 7 * b + 4)
                    nc.tensor.matmul(psum[:, 7, 0:2], avg[:], spread[:], start=True, stop=True).then_inc(group_mm, 1)
                    with pe.Fori(0, QUARTERS) as q:
                        for t in range(TILES):
                            for g in range(2):
                                pe.wait_ge(xn_ready, XN_CREDIT + (b * QUARTERS + q) * 4 * TILES + 4 * t + 2 * g + 2)
                                for m in range(2):
                                    n = 2 * t + m
                                    count = (b * QUARTERS + q) * F_TILES + n + 1
                                    pe.wait_ge(right_used if g else left_ready, count)
                                    bank = LEFT_BANKS + n % RIGHT_BANKS if g else n % LEFT_BANKS
                                    for k in range(2):
                                        last = nc.tensor.matmul(psum[:, bank, :], dct_h[:, k, m * P:(m + 1) * P],
                                                                xn[:, t % 2, g, k, :], start=(k == 0), stop=(k == 1))
                                    last.then_inc(right_full if g else left_full, 1)


def mix_phase(nc, y_dram, z_dram, w, psum):
    with ExitStack() as ctx:
        def sb(name, shape):
            return ctx.enter_context(nc.sbuf_tensor("m_" + name, shape, F32))

        def sem(name):
            return ctx.enter_context(nc.semaphore("m_" + name))

        dct_w = sb("dct_w", [P, 2, HW])
        idct_w = sb("idct_w", [P, 2, HW])
        ident = sb("ident", [P, P])
        block_ones = sb("block_ones", [P, 2])
        ones32 = sb("ones32", [P, P])
        eye32 = sb("eye32", [P, 32])
        head_mask = sb("head_mask", [P, 32])
        spare = sb("spare", [P, 2 * T2])
        one = sb("one", [P, 1])
        wts = sb("wts", [P, 5, P])
        proj = sb("proj", [P, C])
        tap_w = sb("tap_w", [P, TAPS])
        taps = sb("taps", [P, TAPS, P])
        bias = sb("bias", [P, 1])
        rescale = sb("rescale", [P, 1])
        coef = sb("coef", [P, K, W])
        one_minus = sb("one_minus", [P, K, W])
        y_st = sb("y_st", [P, 2, ROWS, 2, C])
        xd = sb("xd", [P, NB, K * K])
        xh = sb("xh", [P, 2, W])
        h1 = sb("h1", [P, ROWS, W + 2])
        xc = sb("xc", [P, K, W])
        base = sb("base", [P, K, W])
        hi = sb("hi", [P, K, W])
        qk = sb("qk", [P, T2, 2, P])
        sq = sb("sq", [P, T2, 2, P])
        norm = sb("norm", [P, 2, 2 * T2])
        rnorm = sb("rnorm", [P, 2, 2 * T2])
        rq = sb("rq", [P, 2 * T2])
        diag_rk = sb("diag_rk", [P, 2 * T2, 32])
        logits = sb("logits", [P, 2 * T2, 32])
        row_max = sb("row_max", [P, 2 * T2])
        row_sum = sb("row_sum", [P, 2 * T2])
        row_inv = sb("row_inv", [P, 2 * T2])
        attn = sb("attn", [P, 2 * T2, P])
        ap = sb("ap", [P, 2 * T2, P])
        v = sb("v", [P, NB, K * K])
        z = sb("z", [P, K, W])
        zt = sb("zt", [P, 2, K, P])
        out = sb("out", [P, 2, 2, K, C])

        consts_loaded = sem("consts_loaded")
        zeroed = sem("zeroed")
        weights_loaded = sem("weights_loaded")
        taps_ready = sem("taps_ready")
        y_loaded = sem("y_loaded")
        coef_loaded = sem("coef_loaded")
        one_minus_ready = sem("one_minus_ready")
        act_full = sem("act_full")
        act_emptied = sem("act_emptied")
        dve_full = sem("dve_full")
        dve_emptied = sem("dve_emptied")
        rooted = sem("rooted")
        rnorm_ready = sem("rnorm_ready")
        rq_ready = sem("rq_ready")
        diag_ready = sem("diag_ready")
        masked = sem("masked")
        max_ready = sem("max_ready")
        shifted = sem("shifted")
        exp_ready = sem("exp_ready")
        sum_ready = sem("sum_ready")
        inv_ready = sem("inv_ready")
        attn_ready = sem("attn_ready")
        xc_ready = sem("xc_ready")
        base_step = sem("base_step")
        hi_step = sem("hi_step")
        conv_full = sem("conv_full")
        tap_step = sem("tap_step")
        conv_emptied = sem("conv_emptied")
        normed = sem("normed")
        z_ready = sem("z_ready")
        z_stored = sem("z_stored")

        def before(order, rnd, name):
            skipped = 0
            if isinstance(rnd, int) and name != ("c2", 3):
                skipped = ACT_IDX["t", 0] - 1
            return rnd * len(order) + order[name] - skipped

        def bank_of(order, rnd, name):
            n = before(order, rnd, name) if isinstance(rnd, int) else order[name]
            return psum[:, n % ACT_BANKS if order is ACT_IDX else ACT_BANKS + n % DVE_BANKS, :]

        def conv_bank(i):
            return psum[:, ACT_BANKS + DVE_BANKS + i % CONV_BANKS, :]

        def act_bank(rnd, *name):
            return bank_of(ACT_IDX, rnd, name)

        def dve_bank(rnd, *name):
            return bank_of(DVE_IDX, rnd, name)

        def act_filled(rnd, *name):
            return before(ACT_IDX, rnd, name) + ACT_CREDIT + 1

        def dve_filled(rnd, *name):
            return before(DVE_IDX, rnd, name) + 1

        def act_has(rnd, *name):
            return before(ACT_IDX, rnd, name) + ACT_BANKS + 1

        def dve_has(rnd, *name):
            return before(DVE_IDX, rnd, name) + DVE_BANKS + 1

        def rows_view(t, r0, n):
            return t[:].rearrange("p w (r k) -> p r w k", k=K)[:, r0:r0 + n]

        with nc.Block() as block:
            @block.sync
            def _(sp):
                for dst, src in ((ident, w["ident"]), (block_ones, w["block_ones"]), (ones32, w["ones32"]),
                                 (eye32, w["eye32"]), (head_mask, w["head_mask"]), (dct_w, w["dct_w"]), (idct_w, w["idct_w"])):
                    sp.dma_start(dst[:], src).then_inc(consts_loaded, 16)
                sp.wait_ge(zeroed, 1)
                for half in range(2):
                    r = slice(half * C, (half + 1) * C)
                    for i, name in enumerate(("c1a", "c2", "wv", "wq", "wk")):
                        sp.dma_start(wts[r, i, r], w[name]).then_inc(weights_loaded, 16)
                    sp.dma_start(proj[r, :], w["proj"]).then_inc(weights_loaded, 16)
                    sp.dma_start(tap_w[r, :], w["taps"]).then_inc(weights_loaded, 16)
                    sp.dma_start(bias[r, :], w["proj_b"].rearrange("(c n) -> c n", n=1)).then_inc(weights_loaded, 16)
                    for h in range(HEADS):
                        sp.dma_start(rescale[half * C + h * DH:half * C + (h + 1) * DH, :],
                                     w["rescale"][h:h + 1].partition_broadcast(DH)).then_inc(weights_loaded, 16)
                def load_y(s, b):
                    sp.wait_ge(act_full, (s * B + b) * ACT_TILES + 1)
                    sp.wait_ge(zeroed, 1)
                    for q in range(2):
                        for half in range(2):
                            sp.dma_start(y_st[:, q, :, half, :],
                                         y_dram[b, bass.ds(s * K + half * P, ROWS), q]
                                         .rearrange("r w c -> w r c")).then_inc(y_loaded, 16)

                with sp.Fori(0, STRIPS) as s:
                    load_y(s, 0)
                    sp.wait_ge(dve_emptied, s * B * DVE_TILES + DVE_BANKS)
                    sp.wait_ge(zeroed, 1)
                    for half in range(2):
                        sp.dma_start(coef[half * C:(half + 1) * C],
                                     w["coef"][bass.ds(s * K + half * P, K), :].rearrange("r w -> (r w)")
                                     .partition_broadcast(C)).then_inc(coef_loaded, 16)
                    with sp.Fori(1, B) as b:
                        load_y(s, b)

            @block.gpsimd
            def _(pool):
                nc.gpsimd.memset(wts[:], 0.0).then_inc(zeroed, 1)
                nc.gpsimd.memset(attn[:], 0.0).then_inc(zeroed, 1)
                nc.gpsimd.memset(ap[:], 0.0).then_inc(zeroed, 1)
                nc.gpsimd.memset(h1[:], 0.0).then_inc(zeroed, 1)
                nc.gpsimd.memset(spare[:], 0.0).then_inc(zeroed, 1)
                nc.gpsimd.memset(one[:], 1.0).then_inc(zeroed, 1)
                nc.gpsimd.memset(hi[:], 0.0).then_inc(hi_step, 1)
                nc.gpsimd.memset(base[:], 0.0).then_inc(base_step, 9)
                nc.gpsimd.memset(xc[:], 0.0).then_inc(xc_ready, 4)
                nc.gpsimd.memset(one_minus[:], 0.0).then_inc(zeroed, 1)
                nc.gpsimd.memset(z[:], 0.0).then_inc(zeroed, 1)
                nc.gpsimd.memset(out[:, 0, 0, 0, 0:1], 0.0).then_inc(z_stored, 1)
                pool.wait_ge(consts_loaded, 7 * 16)
                pool.wait_ge(weights_loaded, 24 * 16)
                pool.wait_ge(zeroed, 8)

                def x_conv(it, i):
                    pool.wait_ge(conv_emptied, it * 4 + CONV_BANKS + i + 1)
                    part = xc[:, 2 * i:2 * i + 2, :].rearrange("p r (w k) -> p r w k", k=K)
                    nc.gpsimd.tensor_tensor(part, part, rows_view(xd, 2 * i, 2), ALU.add).then_inc(xc_ready, 1)
                    rows = slice(2 * i, 2 * i + 2)
                    pool.wait_ge(xc_ready, it * 4 + 4 + i + 1)
                    nc.gpsimd.tensor_tensor(base[:, rows], xc[:, rows], one_minus[:, rows], ALU.mult
                                            ).then_inc(base_step, 1)
                    pool.wait_ge(base_step, it * 8 + 8 + 2 * i + 2)
                    part = base[:, rows, :].rearrange("p r (w k) -> p r w k", k=K)
                    nc.gpsimd.tensor_tensor(part, part, rows_view(xd, 2 * i, 2), ALU.add).then_inc(base_step, 1)

                def x_high(rnd, i):
                    rows = slice(2 * i, 2 * i + 2)
                    pool.wait_ge(act_emptied, act_has(rnd, "c2", i))
                    nc.gpsimd.tensor_tensor(hi[:, rows], hi[:, rows], one_minus[:, rows], ALU.mult
                                            ).then_inc(hi_step, 1)
                    pool.wait_ge(base_step, rnd * 8 + (9 if i == 3 else 8 + 2 * i + 3))
                    pool.wait_ge(hi_step, rnd * 8 + (2 if i == 3 else 2 * i + 4))
                    nc.gpsimd.tensor_tensor(hi[:, rows], hi[:, rows], base[:, rows], ALU.add
                                            ).then_inc(hi_step, 1)

                def strip(it):
                    x_conv(it, 0)
                    x_conv(it, 1)
                    pool.wait_ge(rnorm_ready, it + 1)
                    nc.gpsimd.tensor_tensor(diag_rk[:], rnorm[:, 1, :].unsqueeze(2).to_broadcast([P, 2 * T2, 32]),
                                            eye32[:].unsqueeze(1).to_broadcast([P, 2 * T2, 32]), ALU.mult
                                            ).then_inc(diag_ready, 1)
                    nc.gpsimd.tensor_scalar(rq[:], rnorm[:, 0, :], rescale[:, 0:1], None, ALU.mult
                                            ).then_inc(rq_ready, 1)
                    x_conv(it, 2)
                    for i in range(3):
                        x_high(it, i)
                    x_conv(it, 3)

                with pool.Fori(0, STRIPS) as s:
                    first = pool.snap(s * B)
                    x_high(first, 3)
                    pool.wait_ge(coef_loaded, s * 32 + 32)
                    nc.gpsimd.tensor_tensor(one_minus[:].rearrange("p r w -> p (r w)"),
                                            one[:].to_broadcast([P, K * W]), coef[:].rearrange("p r w -> p (r w)"),
                                            ALU.subtract).then_inc(one_minus_ready, 1)
                    strip(first)
                    with pool.Fori(1, B) as b:
                        it = pool.snap(s * B + b)
                        x_high(it, 3)
                        strip(it)
                x_high(LAST, 3)

            @block.scalar
            def _(act):
                act.wait_ge(zeroed, 8)
                nc.scalar.activation(row_sum[:], spare[:], ACT.Identity).then_inc(act_emptied, ACT_BANKS)
                nc.scalar.activation(row_inv[:], spare[:], ACT.Identity).then_inc(act_full, ACT_CREDIT)
                nc.scalar.activation(row_max[:], spare[:], ACT.Identity).then_inc(conv_emptied, CONV_BANKS)
                z_view = z_dram.rearrange("b q n (g r) c -> b q n g (r c)", g=2)

                def empty(rnd, out_ap, in_ap, func, *name, count=1):
                    act.wait_ge(act_full, act_filled(rnd, *name))
                    nc.scalar.activation(out_ap, in_ap, func).then_inc(act_emptied, count)

                def two_rows(bank):
                    return bank.rearrange("p (r w) -> p r w", r=2)

                def transposed(rnd):
                    for j in range(4):
                        empty(rnd, zt[:, j % 2, 4 * (j // 2):4 * (j // 2) + 4].rearrange("p r c -> p (r c)"),
                              act_bank(rnd, "t", j), ACT.Identity, "t", j)

                def inverse(rnd, tiles):
                    if 0 in tiles:
                        act.wait_ge(z_stored, rnd * 32 + 1)
                    for j in tiles:
                        rows = slice(4 * (j // 2), 4 * (j // 2) + 4)
                        empty(rnd, out[:, j % 2, :, rows, :].rearrange("p g r c -> p r g c"),
                              act_bank(rnd, "idct", j).rearrange("p (r g c) -> p r g c", r=4, g=2),
                              ACT.Identity, "idct", j)

                def store(rnd, b, s):
                    act.wait_ge(act_emptied, act_has(rnd, "idct", 3))
                    for q in range(2):
                        act.dma_start(z_view[b, q, :, :, bass.ds(s * K * C, K * C)],
                                      out[:, q].rearrange("p g r c -> p g (r c)")).then_inc(z_stored, 16)

                def c2(rnd, j):
                    empty(rnd, hi[:, 2 * j:2 * j + 2], two_rows(act_bank(rnd, "c2", j)), ACT.Gelu, "c2", j)

                with act.Fori(0, LAST) as it:
                    c2(it, 3)
                    empty(it, xh[:], two_rows(act_bank(it, "dct", 0)), ACT.Identity, "dct", 0)
                    for j in range(4):
                        act.wait_ge(base_step, it * 8 + 2 * j + 3)
                        empty(it, rows_view(xd, 2 * j, 2),
                              act_bank(it, "dct", j + 1).rearrange("p (r w k) -> p r w k", r=2, k=K),
                              ACT.Identity, "dct", j + 1)
                    empty(it, h1[:, 0:ROWS:ROWS - 1, 1:W + 1], two_rows(act_bank(it, "c1", 0)), ACT.Gelu, "c1", 0)
                    for j in range(4):
                        empty(it, h1[:, 2 * j + 1:2 * j + 3, 1:W + 1], two_rows(act_bank(it, "c1", j + 1)), ACT.Gelu,
                              "c1", j + 1)

                    def q_and_k(j):
                        act.wait_ge(act_full, act_filled(it, "qk", j))
                        pairs = slice(2 * j, 2 * j + 2)
                        nc.scalar.activation(qk[:, pairs].rearrange("p a b c -> p (a b c)"), act_bank(it, "qk", j),
                                             ACT.Identity)
                        nc.scalar.activation(sq[:, pairs].rearrange("p a b c -> p (a b c)"), act_bank(it, "qk", j),
                                             ACT.Square).then_inc(act_emptied, 1)

                    def conv(i):
                        act.wait_ge(tap_step, it * 4 * DVE_TAPS + DVE_TAPS * (i + 1))
                        nc.scalar.activation(xc[:, 2 * i:2 * i + 2], two_rows(conv_bank(i)), ACT.Gelu
                                             ).then_inc(conv_emptied, 1)

                    def softmax_exp(b):
                        act.wait_ge(shifted, it * 2 + b + 1)
                        part = logits[:, b * T2:(b + 1) * T2]
                        nc.scalar.activation(part, part, ACT.Exp).then_inc(exp_ready, 1)

                    for j in range(4):
                        q_and_k(j)
                    conv(0)
                    for j in range(4, 8):
                        q_and_k(j)
                    conv(1)
                    def values(j):
                        empty(it, v[:, 8 * j:8 * j + 8].rearrange("p w k -> p (w k)"), act_bank(it, "v", j),
                              ACT.Identity, "v", j)

                    for j in range(3):
                        values(j)
                    act.wait_ge(dve_emptied, dve_has(it, "norm", 0))
                    nc.scalar.activation(norm[:], norm[:], ACT.Sqrt).then_inc(rooted, 1)
                    values(3)
                    conv(2)
                    softmax_exp(0)
                    transposed(it)
                    inverse(it, (0, 1))
                    softmax_exp(1)
                    inverse(it, (2, 3))
                    for j in range(3):
                        c2(it, j)
                    for j in range(4):
                        act.wait_ge(act_full, act_filled(it, "u", j))
                        for half in range(2):
                            r = slice(half * C, (half + 1) * C)
                            last = nc.scalar.activation(ap[r, 8 * U_BLOCKS[j]:8 * U_BLOCKS[j] + 8, r],
                                                        act_bank(it, "u", j)[r].rearrange("p (n c) -> p n c", n=8),
                                                        ACT.Identity)
                        last.then_inc(act_emptied, 2 if j == 3 else 1)
                    conv(3)
                    prev = (it + (LAST - 1)) % LAST
                    store(it, prev % B, prev // B)
                c2(LAST, 3)
                transposed(LAST)
                inverse(LAST, range(4))
                store(LAST, B - 1, STRIPS - 1)
                act.wait_ge(z_stored, (LAST + 1) * 32 + 1)

            @block.vector
            def _(dve):
                dve.wait_ge(consts_loaded, 7 * 16)
                dve.wait_ge(weights_loaded, 24 * 16)
                for t in range(TAPS):
                    nc.vector.tensor_scalar(taps[:, t, :], ident[:], tap_w[:, t:t + 1], None, ALU.mult
                                            ).then_inc(taps_ready, 1)
                nc.vector.memset(rnorm[:], 0.0).then_inc(dve_emptied, DVE_BANKS)

                def full(rnd, *name):
                    dve.wait_ge(dve_full, dve_filled(rnd, *name))

                def finish_z(rnd):
                    for r in range(2):
                        rows = slice(4 * r, 4 * r + 4)
                        dve.wait_ge(hi_step, rnd * 8 + 3)
                        nc.vector.tensor_tensor(z[:, rows], z[:, rows], hi[:, rows], ALU.add).then_inc(z_ready, 1)

                with dve.Fori(0, LAST) as it:
                    def add_taps(i):
                        bank = conv_bank(i).rearrange("p (r w) -> p r w", r=2)
                        dve.wait_ge(act_emptied, act_has(it, "c1", min(i + 2, 4)))
                        dve.wait_ge(conv_full, it * 4 + i + 1)
                        for n in range(DVE_TAPS):
                            dr, dw = (PE_TAPS + n) // 3, (PE_TAPS + n) % 3
                            if n:
                                dve.wait_ge(tap_step, it * 4 * DVE_TAPS + DVE_TAPS * i + n)
                            nc.vector.scalar_tensor_tensor(out=bank, in0=h1[:, 2 * i + dr:2 * i + dr + 2, dw:dw + W],
                                                           scalar=tap_w[:, PE_TAPS + n:PE_TAPS + n + 1], in1=bank,
                                                           op0=ALU.mult, op1=ALU.add).then_inc(tap_step, 1)

                    def make_logits(b):
                        blocks = slice(b * T2, (b + 1) * T2)
                        part = logits[:, blocks]
                        full(it, "s", b)
                        nc.vector.tensor_tensor(part, dve_bank(it, "s", b).rearrange("p (t e) -> p t e", e=32),
                                                rq[:, blocks].unsqueeze(2).to_broadcast([P, T2, 32]), ALU.mult
                                                ).then_inc(dve_emptied, 1)
                        full(it, "rk", b)
                        dve.wait_ge(dve_emptied, dve_has(it, "s", b))
                        nc.vector.tensor_tensor(part, dve_bank(it, "rk", b).rearrange("p (t e) -> p t e", e=32),
                                                part, ALU.mult).then_inc(dve_emptied, 1)
                        dve.wait_ge(dve_emptied, dve_has(it, "rk", b))
                        nc.vector.tensor_tensor(part, part, head_mask[:].unsqueeze(1).to_broadcast([P, T2, 32]),
                                                ALU.add).then_inc(masked, 1)
                        dve.wait_ge(masked, it * 2 + b + 1)
                        nc.vector.tensor_reduce(row_max[:, blocks], part, AX.X, ALU.max).then_inc(max_ready, 1)
                        dve.wait_ge(max_ready, it * 2 + b + 1)
                        nc.vector.tensor_tensor(part, part, row_max[:, blocks].unsqueeze(2).to_broadcast([P, T2, 32]),
                                                ALU.subtract).then_inc(shifted, 1)

                    def normalise(b):
                        blocks = slice(b * T2, (b + 1) * T2)
                        part = logits[:, blocks]
                        count = it * 2 + b + 1
                        dve.wait_ge(exp_ready, count)
                        nc.vector.tensor_reduce(row_sum[:, blocks], part, AX.X, ALU.add).then_inc(sum_ready, 1)
                        dve.wait_ge(sum_ready, count)
                        nc.vector.reciprocal(row_inv[:, blocks], row_sum[:, blocks]).then_inc(inv_ready, 1)
                        dve.wait_ge(inv_ready, count)
                        nc.vector.tensor_tensor(part, part, row_inv[:, blocks].unsqueeze(2).to_broadcast([P, T2, 32]),
                                                ALU.mult).then_inc(normed, 1)
                        dve.wait_ge(normed, count)
                        for j in range(4):
                            r = slice(32 * j, 32 * j + 32)
                            nc.vector.tensor_copy(attn[r, blocks, r], logits[r, blocks]).then_inc(attn_ready, 1)

                    add_taps(0)
                    finish_z(it)
                    add_taps(1)
                    add_taps(2)
                    full(it, "norm", 0)
                    nc.vector.tensor_scalar(norm[:].rearrange("p a b -> p (a b)"), dve_bank(it, "norm", 0)[:, 0:64],
                                            1e-24, None, ALU.max).then_inc(dve_emptied, 1)
                    dve.wait_ge(rooted, it + 1)
                    nc.vector.reciprocal(rnorm[:].rearrange("p a b -> p (a b)"), norm[:].rearrange("p a b -> p (a b)")
                                         ).then_inc(rnorm_ready, 1)
                    dve.wait_ge(rq_ready, it + 1)
                    make_logits(0)
                    make_logits(1)
                    normalise(0)
                    normalise(1)
                    add_taps(3)
                    for q in range(4):
                        part = slice(64 * q, 64 * q + 64)
                        full(it, "low", q)
                        nc.vector.scalar_tensor_tensor(out=z[:, :, part],
                                                       in0=dve_bank(it, "low", q).rearrange("p (r w) -> p r w", r=K),
                                                       scalar=bias[:, 0:1], in1=coef[:, :, part],
                                                       op0=ALU.add, op1=ALU.mult).then_inc(dve_emptied, 1)
                    dve.wait_ge(dve_emptied, dve_has(it, "low", 3))
                finish_z(LAST)

            @block.tensor
            def _(pe):
                pe.wait_ge(consts_loaded, 7 * 16)
                pe.wait_ge(weights_loaded, 24 * 16)
                pe.wait_ge(taps_ready, TAPS)
                pe.wait_ge(zeroed, 8)
                c1a_w, c2_w, v_w = (wts[:, i, :] for i in range(3))
                proj_w = proj[:]
                qk_w = wts[:, 3:5, :].rearrange("p a b -> p (a b)")

                def act_tile(rnd, *name):
                    pe.wait_ge(act_emptied, before(ACT_IDX, rnd, name) + 1)
                    return act_bank(rnd, *name)

                def dve_tile(rnd, *name):
                    pe.wait_ge(dve_emptied, before(DVE_IDX, rnd, name) + 1)
                    return dve_bank(rnd, *name)

                def transpose_z(rnd):
                    for j in range(4):
                        pe.wait_ge(z_ready, rnd * 2 + j // 2 + 1)
                        bank = act_tile(rnd, "t", j)
                        for r in range(4):
                            last = nc.tensor.transpose(bank[:, r * P:(r + 1) * P],
                                                       z[:, 4 * (j // 2) + r, j % 2:W:2], ident[:])
                        last.then_inc(act_full, 1)

                def inverse_dct(rnd):
                    for j in range(4):
                        rows = slice(4 * (j // 2), 4 * (j // 2) + 4)
                        pe.wait_ge(act_emptied, act_has(rnd, "t", j))
                        nc.tensor.matmul(act_tile(rnd, "idct", j), idct_w[:, j % 2, :],
                                         zt[:, j % 2, rows].rearrange("p r c -> p (r c)"),
                                         start=True, stop=True).then_inc(act_full, 1)

                def c2(rnd, i):
                    pe.wait_ge(xc_ready, rnd * 4 + 4 + (0 if i == 3 else i + 1))
                    nc.tensor.matmul(act_tile(rnd, "c2", i), c2_w, xc[:, 2 * i:2 * i + 2, :],
                                     start=True, stop=True).then_inc(act_full, 1)

                with pe.Fori(0, LAST) as it:
                    def conv(i):
                        pe.wait_ge(act_emptied, act_has(it, "c1", min(i + 2, 4)))
                        pe.wait_ge(conv_emptied, it * 4 + i + 1)
                        bank = conv_bank(i)
                        for t in range(PE_TAPS):
                            dr, dw = t // 3, t % 3
                            last = nc.tensor.matmul(bank, taps[:, t, :], h1[:, 2 * i + dr:2 * i + dr + 2, dw:dw + W],
                                                    start=(t == 0), stop=(t == PE_TAPS - 1))
                        last.then_inc(conv_full, 1)

                    pe.wait_ge(y_loaded, it * 64 + 64)
                    c2(it, 3)
                    for j in range(5):
                        bank = act_tile(it, "dct", j)
                        for n, row in enumerate((0, ROWS - 1) if j == 0 else (2 * j - 1, 2 * j)):
                            for q in range(2):
                                last = nc.tensor.matmul(bank[:, n * W + q:(n + 1) * W:2],
                                                        y_st[:, q, row].rearrange("p g c -> p (g c)"), dct_w[:, q, :],
                                                        start=True, stop=True)
                        last.then_inc(act_full, 1)
                    def c1(j):
                        pe.wait_ge(act_emptied, act_has(it, "dct", j))
                        nc.tensor.matmul(act_tile(it, "c1", j), c1a_w, xh[:] if j == 0 else rows_view(xd, 2 * j - 2, 2),
                                         start=True, stop=True).then_inc(act_full, 1)

                    def q_and_k(j):
                        bank = act_tile(it, "qk", j)
                        for t in range(2):
                            pair = 2 * j + t
                            last = nc.tensor.matmul(bank[:, t * 256:(t + 1) * 256],
                                                    xd[:, 2 * pair:2 * pair + 2].rearrange("p w k -> p (w k)"), qk_w,
                                                    start=True, stop=True)
                        last.then_inc(act_full, 1)

                    def norms(j):
                        pe.wait_ge(act_emptied, act_has(it, "qk", j))
                        for t in (2 * j, 2 * j + 1):
                            for q in range(2):
                                last = nc.tensor.matmul(norm_bank[:, q, :, t], sq[:, t, q, :], block_ones[:],
                                                        start=True, stop=True)
                        return last

                    def values(j):
                        nc.tensor.matmul(act_tile(it, "v", j), v_w, xd[:, 8 * j:8 * j + 8].rearrange("p w k -> p (w k)"),
                                         start=True, stop=True).then_inc(act_full, 1)

                    def scores(b):
                        pos = slice(64 * b, 64 * b + 64)
                        for t in range(T2):
                            for g in range(4):
                                ch = slice(32 * g, 32 * g + 32)
                                last = nc.tensor.matmul(s_banks[b][ch, 32 * t:32 * t + 32], qk[pos, t, 0, ch],
                                                        qk[pos, t, 1, ch], start=True, stop=True)
                        last.then_inc(dve_full, 1)

                    def k_norms(b):
                        nc.tensor.matmul(dve_tile(it, "rk", b), ones32[:],
                                         diag_rk[:, b * T2:(b + 1) * T2].rearrange("p t e -> p (t e)"),
                                         start=True, stop=True).then_inc(dve_full, 1)

                    for j in range(4):
                        c1(j)
                    conv(0)
                    c1(4)
                    for j in range(4):
                        q_and_k(j)
                    conv(1)
                    norm_bank = dve_tile(it, "norm", 0)[:, 0:64].rearrange("p (q b t) -> p q b t", q=2, b=2)
                    for j in range(4, 8):
                        q_and_k(j)
                        norms(j - 4)
                    conv(2)
                    norms(4)
                    values(0)
                    norms(5)
                    values(1)
                    norms(6)
                    values(2)
                    norms(7).then_inc(dve_full, 1)
                    s_banks = [dve_tile(it, "s", 0)]
                    values(3)
                    scores(0)
                    conv(3)
                    pe.wait_ge(diag_ready, it + 1)
                    s_banks.append(dve_tile(it, "s", 1))
                    k_norms(0)
                    scores(1)
                    k_norms(1)
                    transpose_z(it)
                    inverse_dct(it)
                    for i in range(3):
                        c2(it, i)
                    for j in range(4):
                        pe.wait_ge(attn_ready, it * 8 + 4 * (U_BLOCKS[j] // 2) + 4)
                        bank = act_tile(it, "u", j)
                        for n in range(8):
                            last = nc.tensor.matmul(bank[:, n * C:(n + 1) * C], attn[:, 8 * U_BLOCKS[j] + n, :], proj_w,
                                                    start=True, stop=True)
                        last.then_inc(act_full, 2 if j == 3 else 1)
                    for q in range(4):
                        pe.wait_ge(act_emptied, act_has(it, "u", 1 if q < 2 else 3) + (q >= 2))
                        bank = dve_tile(it, "low", q).rearrange("p (r w) -> p r w", r=K)
                        for n in range(8):
                            wb = 8 * q + n
                            last = nc.tensor.matmul(bank[:, :, n * K:(n + 1) * K], ap[:, (wb % 2) * T2 + wb // 2, :],
                                                    v[:, wb, :], start=True, stop=True)
                        last.then_inc(dve_full, 1)
                c2(LAST, 3)
                transpose_z(LAST)
                inverse_dct(LAST)


def inverse_phase(nc, x, z_dram, idct, out, psum):
    with ExitStack() as ctx:
        def sb(name, shape):
            return ctx.enter_context(nc.sbuf_tensor("i_" + name, shape, F32))

        def sem(name):
            return ctx.enter_context(nc.semaphore("i_" + name))

        idct_h = sb("idct_h", [P, 2, H])
        z_sb = sb("z_sb", [P, 2, 2, 2, WT * C])
        x_sb = sb("x_sb", [P, 2, 2, 2, WT * C])
        o_sb = sb("o_sb", [P, 2, 2, 2, WT * C])

        consts_loaded = sem("consts_loaded")
        z_loaded = [sem(f"z_loaded{i}") for i in range(2)]
        x_loaded = [sem(f"x_loaded{i}") for i in range(2)]
        psum_full = sem("psum_full")
        psum_used = sem("psum_used")
        added = sem("added")
        stored = [sem(f"stored{i}") for i in range(2)]
        x_view = x.rearrange("b (k p) g w c -> b p k g (w c)", p=P)
        out_view = out.rearrange("b (k p) g w c -> b p k g (w c)", p=P)

        with nc.Block() as block:
            @block.sync
            def _(sp):
                sp.dma_start(idct_h[:], idct.rearrange("(k p) n -> p k n", p=P)).then_inc(consts_loaded, 16)
                with sp.Fori(0, B) as b:
                    with sp.Fori(0, I_STEPS) as i:
                        for slot in range(2):
                            sp.wait_ge(psum_used, (b * I_STEPS + i) * 4 + 2 * slot + 2)
                            sp.wait_ge(consts_loaded, 16)
                            for k in range(2):
                                for q in range(2):
                                    sp.dma_start(z_sb[:, slot, k, q].rearrange("p (w c) -> p w c", c=C),
                                                 z_dram[b, q, bass.ds(i * 2 * WT + slot * WT, WT), k * P:(k + 1) * P, :]
                                                 .rearrange("w k c -> k w c")).then_inc(z_loaded[slot], 16)
                            for k in range(2):
                                sp.dma_start(x_sb[:, slot, k],
                                             x_view[b, :, k, :, bass.ds((i * 2 + slot) * WT * C, WT * C)]
                                             ).then_inc(x_loaded[slot], 16)

            @block.tensor
            def _(pe):
                pe.wait_ge(consts_loaded, 16)
                with pe.Fori(0, B * I_STEPS) as it:
                    for slot in range(2):
                        pe.wait_ge(z_loaded[slot], it * 64 + 64)
                        for m in range(2):
                            n = 2 * slot + m
                            pe.wait_ge(psum_used, it * 4 + n + 1)
                            for q in range(2):
                                for k in range(2):
                                    last = nc.tensor.matmul(psum[:, 2 * n + q, :], idct_h[:, k, m * P:(m + 1) * P],
                                                            z_sb[:, slot, k, q, :], start=(k == 0), stop=(k == 1))
                            last.then_inc(psum_full, 1)

            @block.vector
            def _(dve):
                nc.vector.memset(o_sb[:, 0, 0, 0, 0:2], 0.0).then_inc(psum_used, 4)
                for slot in range(2):
                    nc.vector.memset(o_sb[:, slot, 1, 0, 0:2], 0.0).then_inc(stored[slot], 1)
                with dve.Fori(0, B * I_STEPS) as it:
                    for slot in range(2):
                        dve.wait_ge(x_loaded[slot], it * 32 + 32)
                        dve.wait_ge(stored[slot], it * 32 + 1)
                        for m in range(2):
                            n = 2 * slot + m
                            even, odd = psum[:, 2 * n, :], psum[:, 2 * n + 1, :]
                            dve.wait_ge(psum_full, it * 4 + n + 1)
                            for g in range(2):
                                last = nc.vector.tensor_tensor(o_sb[:, slot, m, g], even, x_sb[:, slot, m, g], ALU.add)
                            last.then_inc(added, 1)
                            dve.wait_ge(added, it * 4 + n + 1)
                            for g, op in enumerate((ALU.add, ALU.subtract)):
                                last = nc.vector.tensor_tensor(o_sb[:, slot, m, g], o_sb[:, slot, m, g], odd, op)
                            last.then_inc(psum_used, 1)

            @block.scalar
            def _(act):
                with act.Fori(0, B) as b:
                    with act.Fori(0, I_STEPS) as i:
                        for slot in range(2):
                            act.wait_ge(psum_used, (b * I_STEPS + i) * 4 + 2 * slot + 6)
                            for k in range(2):
                                act.dma_start(out_view[b, :, k, :, bass.ds((i * 2 + slot) * WT * C, WT * C)],
                                              o_sb[:, slot, k]).then_inc(stored[slot], 16)
                for slot in range(2):
                    act.wait_ge(stored[slot], B * I_STEPS * 32 + 1)


def build(nc, args, out):
    y_dram = nc.dram_tensor("y_dram", (B, H + 2, 2, HW, C), F32, kind="Internal").ap()
    z_dram = nc.dram_tensor("z_dram", (B, 2, HW, H, C), F32, kind="Internal").ap()
    with nc.psum_tensor("psum", [P, 8, BANK], F32) as psum:
        forward_phase(nc, args["x"], y_dram, args["dct"], args["group_avg"], psum)
        mix_phase(nc, y_dram, z_dram, args, psum)
        inverse_phase(nc, args["x"], z_dram, args["idct"], out, psum)


def shape_constants():
    import numpy as np

    n = np.arange(H)
    cos = np.cos(np.pi * (2 * n[None, :] + 1) * n[:, None] / (2 * H))
    wk = np.ones(H)
    wk[0] = 0.5
    dct = np.ascontiguousarray((2.0 * cos).T).astype(np.float32)
    idct = (wk[:, None] * cos / H).astype(np.float32)
    p = np.arange(P)
    return {
        "dct": dct,
        "idct": idct,
        "dct_w": dct[:HW].reshape(HW, HW, 2).transpose(0, 2, 1),
        "idct_w": idct[:, :HW].reshape(HW, 2, HW),
        "group_avg": ((p[:, None] // GROUP_ROWS == p[None, :] // GROUP_ROWS) / GROUP_ROWS).astype(np.float32),
        "ident": np.eye(P, dtype=np.float32),
        "block_ones": (p[:, None] // C == np.arange(2)[None, :]).astype(np.float32),
        "ones32": (p[:, None] // 32 == p[None, :] // 32).astype(np.float32),
        "eye32": (p[:, None] % 32 == np.arange(32)[None, :]).astype(np.float32),
        "head_mask": np.where(p[:, None] % 32 // DH == np.arange(32)[None, :] // DH, 0, -1e30).astype(np.float32),
    }


def kernel(x, L0_conv_Wq, L0_conv_Wk, L0_conv_Wv, L0_conv_rescale, L0_conv_proj_w, L0_conv_proj_b,
           L0_conv_c1a_w, L0_conv_c1b_w, L0_conv_c2_w, L0_conv_coef_emb):
    import numpy as np
    import concourse.bacc as bacc
    from concourse.bass_utils import run_bass_kernel_spmd

    def mirror(a):
        a = np.asarray(a).reshape(B, H, 2, HW, C)
        return np.stack([a[:, :, 0], a[:, :, 1, ::-1]], axis=2)

    arrays = {
        "x": mirror(x), "wq": L0_conv_Wq, "wk": L0_conv_Wk, "wv": L0_conv_Wv, "proj": L0_conv_proj_w,
        "proj_b": L0_conv_proj_b, "rescale": np.asarray(L0_conv_rescale).reshape(HEADS, 1),
        "c1a": np.asarray(L0_conv_c1a_w).reshape(C, C).T, "c2": np.asarray(L0_conv_c2_w).reshape(C, C).T,
        "taps": np.asarray(L0_conv_c1b_w).reshape(C, TAPS), "coef": L0_conv_coef_emb,
        **shape_constants(),
    }
    arrays = {name: np.ascontiguousarray(a) for name, a in arrays.items()}
    nc = bacc.Bacc("TRN2", target_bir_lowering=False, num_devices=1)
    args = {name: nc.dram_tensor(name, a.shape, mybir.dt.from_np(a.dtype), kind="ExternalInput").ap()
            for name, a in arrays.items()}
    out = nc.dram_tensor("result", (B, H, 2, HW, C), F32, kind="ExternalOutput").ap()
    build(nc, args, out)
    result = run_bass_kernel_spmd(nc, [arrays], core_ids=[0]).results[0]["result"]
    return mirror(result).reshape(B, H, W, C)
```

```python
from contextlib import ExitStack

import concourse.bass as bass
from concourse import mybir

F32 = mybir.dt.float32
ALU = mybir.AluOpType
ACT = mybir.ActivationFunctionType
AX = mybir.AxisListType

P = 128
B, H, W, C = 4, 256, 256, 64
GROUP_ROWS = 8
K = 8
HEADS, DH = 4, 16
BANK = 512

HW = W // 2
COLS = HW * C
QUARTERS = 4
QCOLS = COLS // QUARTERS
TILES = QCOLS // BANK
BATCH = 2
F_TILES = 2 * TILES
XN_CREDIT = 4 * TILES * QUARTERS
LEFT_BANKS, RIGHT_BANKS = 2, 4

STRIPS = H // 2 // K
ROWS = K + 2
NB = W // K
T2 = NB // 2
TAPS = 9
PE_TAPS = (1, 1, 2, 1)
DVE_TAPS = TAPS * 4 - sum(PE_TAPS)


def tap_steps(i, n=0):
    return sum(TAPS - taps for taps in PE_TAPS[:i]) + n


ACT_ORDER = ([("c2", 3)] + [("dct", j) for j in range(5)] + [("c1", j) for j in range(5)] + [("qk", j) for j in range(8)]
             + [("v", j) for j in range(4)] + [("t", j) for j in range(4)] + [("idct", j) for j in range(4)]
             + [("c2", j) for j in range(2)] + [("av", j) for j in range(4)] + [("c2", 2), ("none", 0)])
DVE_ORDER = ([("norm", 0), ("s", 0), ("rk", 0), ("s", 1), ("rk", 1)] + [("low", j) for j in range(4)])
ACT_TILES, DVE_TILES = len(ACT_ORDER), len(DVE_ORDER)
ACT_BANKS, DVE_BANKS, CONV_BANKS = 3, 3, 2
ACT_IDX = {name: i for i, name in enumerate(ACT_ORDER)}
DVE_IDX = {name: i for i, name in enumerate(DVE_ORDER)}
LAST = STRIPS * B
ACT_CREDIT = ACT_TILES - 5
assert ACT_TILES % ACT_BANKS == 0 and DVE_TILES % DVE_BANKS == 0

WT = 8
SLOTS = 4
I_STEPS = HW // WT // SLOTS


def forward_phase(nc, x, y_dram, dct, group_avg, psum):
    with ExitStack() as ctx:
        def sb(name, shape):
            return ctx.enter_context(nc.sbuf_tensor("f_" + name, shape, F32))

        def sem(name):
            return ctx.enter_context(nc.semaphore("f_" + name))

        x_sb = sb("x_sb", [P, 2, 2, COLS])
        xn = sb("xn", [P, 2, 2, 2, BANK])
        left = sb("left", [P, 4, BANK])
        y_sb = sb("y_sb", [P, 2, 2, 2, BATCH * BANK])
        dct_h = sb("dct_h", [P, 2, H])
        avg = sb("avg", [P, P])
        zero_row = sb("zero_row", [P, W * C // P])
        stats = sb("stats", [P, 2, 2 * COLS // BANK, 6])
        mean_var = sb("mean_var", [P, 2, 2])
        group_mean = sb("group_mean", [P, 2])
        spread = sb("spread", [P, 2])
        eps = sb("eps", [P, 1])
        std = sb("std", [P, 2])
        rstd = sb("rstd", [P, 2])
        shift = sb("shift", [P, 2])

        consts_loaded = sem("consts_loaded")
        x_loaded = [sem(f"x_loaded{q}") for q in range(QUARTERS)]
        zeroed = sem("zeroed")
        stats_done = sem("stats_done")
        group_mm = sem("group_mm")
        small = sem("small")
        std_done = sem("std_done")
        xn_ready = sem("xn_ready")
        left_full = sem("left_full")
        left_ready = sem("left_ready")
        right_full = sem("right_full")
        right_used = sem("right_used")
        y_stored = [sem(f"y_stored{i}") for i in range(2)]
        pad_stored = sem("pad_stored")
        x_view = x.rearrange("b (k p) g w c -> b p k g (w c)", p=P)
        y_rows = y_dram.rearrange("b h g w c -> b h g (w c)")

        with nc.Block() as block:
            @block.sync
            def _(sp):
                sp.dma_start(dct_h[:], dct.rearrange("(k p) n -> p k n", p=P)).then_inc(consts_loaded, 16)
                sp.dma_start(avg[:], group_avg).then_inc(consts_loaded, 16)
                sp.wait_ge(zeroed, 1)
                for b in range(B):
                    for row in (0, H + 1):
                        sp.dma_start(y_rows[b, row].rearrange("g (p n) -> (g p) n", p=P // 2), zero_row[:]
                                     ).then_inc(pad_stored, 16)
                with sp.Fori(0, B) as b:
                    with sp.Fori(0, QUARTERS) as q:
                        for slot in range(2):
                            sp.wait_ge(right_used, RIGHT_BANKS + (b * QUARTERS + q) * F_TILES + 2 * (slot + 1) * BATCH)
                            sp.wait_ge(zeroed, 1)
                            for m in range(2):
                                sp.dma_start(y_rows[b, 1 + m * P:1 + (m + 1) * P, :,
                                                    bass.ds(q * QCOLS + slot * BATCH * BANK, BATCH * BANK)],
                                             y_sb[:, slot, m]).then_inc(y_stored[slot], 16)
                sp.wait_ge(pad_stored, 2 * B * 16)
                for slot in range(2):
                    sp.wait_ge(y_stored[slot], B * QUARTERS * 32 + 1)

            @block.gpsimd
            def _(pool):
                with pool.Fori(0, B) as b:
                    for q in range(QUARTERS):
                        pool.wait_ge(xn_ready, b * XN_CREDIT + (q + 1) * 4 * TILES)
                        for k in range(2):
                            pool.dma_start(x_sb[:, k, :, q * QCOLS:(q + 1) * QCOLS],
                                           x_view[b, :, k, :, q * QCOLS:(q + 1) * QCOLS]).then_inc(x_loaded[q], 16)

            @block.vector
            def _(dve):
                nc.vector.memset(zero_row[:], 0.0).then_inc(zeroed, 1)
                nc.vector.memset(eps[:], 1e-5).then_inc(zeroed, 1)
                nc.vector.memset(xn[:, 0, 0, 0, 0:2], 0.0).then_inc(xn_ready, XN_CREDIT)
                nc.vector.memset(left[:, 0, 0:2], 0.0).then_inc(left_ready, LEFT_BANKS)
                nc.vector.memset(left[:, 1, 0:2], 0.0).then_inc(right_full, 4)
                nc.vector.memset(left[:, 2, 0:2], 0.0).then_inc(right_used, RIGHT_BANKS)
                for slot in range(2):
                    nc.vector.memset(y_sb[:, slot, 0, 0, 0:2], 0.0).then_inc(y_stored[slot], 1)

                def row_stats(b, q):
                    dve.wait_ge(x_loaded[q], b * 32 + 32)
                    for k in range(2):
                        for g in range(2):
                            for t in range(q * TILES, (q + 1) * TILES):
                                last = nc.vector.bn_stats(stats[:, k, g * (COLS // BANK) + t, :],
                                                          x_sb[:, k, g, t * BANK:(t + 1) * BANK])
                    if q == QUARTERS - 1:
                        last.then_inc(stats_done, 1)

                def group_stats(b):
                    dve.wait_ge(stats_done, 2 * b + 1)
                    nc.vector.memset(spread[:], 0.0)
                    for k in range(2):
                        last = nc.vector.bn_aggr(mean_var[:, k, :], stats[:, k, :, :])
                    last.then_inc(stats_done, 1)
                    dve.wait_ge(group_mm, 2 * b + 1)
                    nc.vector.tensor_copy(group_mean[:], psum[:, 6, 0:2]).then_inc(small, 1)
                    dve.wait_ge(small, 7 * b + 1)
                    nc.vector.tensor_tensor(spread[:], mean_var[:, :, 0], group_mean[:], ALU.subtract
                                            ).then_inc(small, 1)
                    dve.wait_ge(small, 7 * b + 2)
                    nc.vector.tensor_tensor(spread[:], spread[:], spread[:], ALU.mult).then_inc(small, 1)
                    dve.wait_ge(small, 7 * b + 3)
                    nc.vector.tensor_tensor(spread[:], spread[:], mean_var[:, :, 1], ALU.add).then_inc(small, 1)
                    dve.wait_ge(std_done, b + 1)
                    nc.vector.reciprocal(rstd[:], std[:]).then_inc(small, 1)
                    dve.wait_ge(small, 7 * b + 5)
                    nc.vector.tensor_tensor(shift[:], group_mean[:], rstd[:], ALU.mult).then_inc(small, 1)
                    dve.wait_ge(small, 7 * b + 6)
                    nc.vector.tensor_scalar(shift[:], shift[:], -1.0, None, ALU.mult).then_inc(small, 1)

                def add_sides(b, q):
                    for slot in range(2):
                        dve.wait_ge(y_stored[slot], (b * QUARTERS + q) * 32 + 1)
                        for j in range(BATCH):
                            for m in range(2):
                                n = 2 * (slot * BATCH + j) + m
                                count = (b * QUARTERS + q) * F_TILES + n + 1
                                dve.wait_ge(right_full, 4 + count)
                                dve.wait_ge(left_ready, LEFT_BANKS + count)
                                cols = slice(j * BANK, (j + 1) * BANK)
                                right = psum[:, LEFT_BANKS + n % RIGHT_BANKS, :]
                                nc.vector.tensor_tensor(y_sb[:, slot, m, 0, cols], left[:, n % 4, :], right, ALU.add)
                                nc.vector.tensor_tensor(y_sb[:, slot, m, 1, cols], left[:, n % 4, :], right,
                                                        ALU.subtract).then_inc(right_used, 1)

                for q in range(QUARTERS):
                    row_stats(0, q)
                with dve.Fori(0, B - 1) as b:
                    group_stats(b)
                    for q in range(QUARTERS):
                        add_sides(b, q)
                        if q:
                            row_stats(b + 1, q - 1)
                    row_stats(b + 1, QUARTERS - 1)
                group_stats(B - 1)
                with dve.Fori(0, QUARTERS) as q:
                    add_sides(B - 1, q)

            @block.scalar
            def _(act):
                act.wait_ge(zeroed, 2)
                with act.Fori(0, B) as b:
                    act.wait_ge(group_mm, 2 * b + 2)
                    nc.scalar.activation(std[:], psum[:, 7, 0:2], ACT.Sqrt, bias=eps[:, 0:1]).then_inc(std_done, 1)
                    act.wait_ge(small, 7 * b + 7)
                    with act.Fori(0, QUARTERS) as q:
                        def normalise(t):
                            act.wait_ge(right_full, (b * QUARTERS + q) * F_TILES + 2 * t + 2)
                            for g in range(2):
                                for k in range(2):
                                    nc.scalar.activation(
                                        xn[:, t % 2, g, k, :], x_sb[:, k, g, bass.ds(q * QCOLS + t * BANK, BANK)],
                                        ACT.Identity, bias=shift[:, k:k + 1], scale=rstd[:, k:k + 1]
                                    ).then_inc(xn_ready, 1)

                        def keep_left(t):
                            for m in range(2):
                                n = 2 * t + m
                                act.wait_ge(left_full, (b * QUARTERS + q) * F_TILES + n + 1)
                                act.wait_ge(right_used, (b * QUARTERS + q) * F_TILES + n + 1)
                                nc.scalar.activation(left[:, n % 4, :], psum[:, n % LEFT_BANKS, :], ACT.Identity
                                                     ).then_inc(left_ready, 1)

                        normalise(0)
                        for t in range(1, TILES):
                            normalise(t)
                            keep_left(t - 1)
                        keep_left(TILES - 1)

            @block.tensor
            def _(pe):
                pe.wait_ge(consts_loaded, 32)
                with pe.Fori(0, B) as b:
                    pe.wait_ge(stats_done, 2 * b + 2)
                    nc.tensor.matmul(psum[:, 6, 0:2], avg[:], mean_var[:, :, 0], start=True, stop=True
                                     ).then_inc(group_mm, 1)
                    pe.wait_ge(small, 7 * b + 4)
                    nc.tensor.matmul(psum[:, 7, 0:2], avg[:], spread[:], start=True, stop=True).then_inc(group_mm, 1)
                    with pe.Fori(0, QUARTERS) as q:
                        for t in range(TILES):
                            for g in range(2):
                                pe.wait_ge(xn_ready, XN_CREDIT + (b * QUARTERS + q) * 4 * TILES + 4 * t + 2 * g + 2)
                                for m in range(2):
                                    n = 2 * t + m
                                    count = (b * QUARTERS + q) * F_TILES + n + 1
                                    pe.wait_ge(right_used if g else left_ready, count)
                                    bank = LEFT_BANKS + n % RIGHT_BANKS if g else n % LEFT_BANKS
                                    for k in range(2):
                                        last = nc.tensor.matmul(psum[:, bank, :], dct_h[:, k, m * P:(m + 1) * P],
                                                                xn[:, t % 2, g, k, :], start=(k == 0), stop=(k == 1))
                                    last.then_inc(right_full if g else left_full, 1)


def mix_phase(nc, y_dram, z_dram, w, psum):
    with ExitStack() as ctx:
        def sb(name, shape):
            return ctx.enter_context(nc.sbuf_tensor("m_" + name, shape, F32))

        def sem(name):
            return ctx.enter_context(nc.semaphore("m_" + name))

        dct_w = sb("dct_w", [P, 2, HW])
        idct_w = sb("idct_w", [P, 2, HW])
        ident = sb("ident", [P, P])
        block_ones = sb("block_ones", [P, 2])
        ones32 = sb("ones32", [P, P])
        eye32 = sb("eye32", [P, 32])
        head_mask = sb("head_mask", [P, 32])
        spare = sb("spare", [P, 2 * T2])
        one = sb("one", [P, 1])
        wts = sb("wts", [P, 6, P])
        tap_w = sb("tap_w", [P, TAPS])
        taps = sb("taps", [P, TAPS, P])
        bias = sb("bias", [P, 1])
        rescale = sb("rescale", [P, 1])
        coef = sb("coef", [P, K, W])
        one_minus = sb("one_minus", [P, K, W])
        y_st = sb("y_st", [P, 2, ROWS, 2, C])
        xd = sb("xd", [P, NB, K * K])
        xh = sb("xh", [P, 2, W])
        h1 = sb("h1", [P, ROWS, W + 2])
        xc = sb("xc", [P, K, W])
        base = sb("base", [P, K, W])
        hi = sb("hi", [P, K, W])
        qk = sb("qk", [P, T2, 2, P])
        sq = sb("sq", [P, T2, 2, P])
        norm = sb("norm", [P, 2, 2 * T2])
        rnorm = sb("rnorm", [P, 2, 2 * T2])
        rq = sb("rq", [P, 2 * T2])
        diag_rk = sb("diag_rk", [P, 2 * T2, 32])
        logits = sb("logits", [P, 2 * T2, 32])
        row_max = sb("row_max", [P, 2 * T2])
        row_sum = sb("row_sum", [P, 2 * T2])
        row_inv = sb("row_inv", [P, 2 * T2])
        probs_t = sb("probs_t", [P, 2 * T2, 32])
        attn = sb("attn", [P, 2 * T2, P])
        av = sb("av", [P, K, NB, K])
        v = sb("v", [P, NB, K * K])
        z = sb("z", [P, K, W])
        zt = sb("zt", [P, 2, K, P])
        out = sb("out", [P, 2, 2, K, C])

        consts_loaded = sem("consts_loaded")
        wts_zeroed = sem("wts_zeroed")
        zeroed = sem("zeroed")
        weights_loaded = sem("weights_loaded")
        taps_ready = sem("taps_ready")
        y_loaded = sem("y_loaded")
        coef_loaded = sem("coef_loaded")
        one_minus_ready = sem("one_minus_ready")
        act_full = sem("act_full")
        act_emptied = sem("act_emptied")
        dve_full = sem("dve_full")
        dve_emptied = sem("dve_emptied")
        rooted = sem("rooted")
        rnorm_ready = sem("rnorm_ready")
        rq_ready = sem("rq_ready")
        diag_ready = sem("diag_ready")
        masked = sem("masked")
        max_ready = sem("max_ready")
        shifted = sem("shifted")
        exp_ready = sem("exp_ready")
        sum_ready = sem("sum_ready")
        inv_ready = sem("inv_ready")
        attn_ready = sem("attn_ready")
        xc_ready = sem("xc_ready")
        base_step = sem("base_step")
        hi_step = sem("hi_step")
        conv_full = sem("conv_full")
        tap_step = sem("tap_step")
        conv_emptied = sem("conv_emptied")
        normed = sem("normed")
        turned = sem("turned")
        z_ready = sem("z_ready")
        z_stored = sem("z_stored")

        def before(order, rnd, name):
            skipped = 0
            if isinstance(rnd, int) and name != ("c2", 3):
                skipped = ACT_IDX["t", 0] - 1
            return rnd * len(order) + order[name] - skipped

        def bank_of(order, rnd, name):
            n = before(order, rnd, name) if isinstance(rnd, int) else order[name]
            return psum[:, n % ACT_BANKS if order is ACT_IDX else ACT_BANKS + n % DVE_BANKS, :]

        def conv_bank(i):
            return psum[:, ACT_BANKS + DVE_BANKS + i % CONV_BANKS, :]

        def act_bank(rnd, *name):
            return bank_of(ACT_IDX, rnd, name)

        def dve_bank(rnd, *name):
            return bank_of(DVE_IDX, rnd, name)

        def act_filled(rnd, *name):
            return before(ACT_IDX, rnd, name) + ACT_CREDIT + 1

        def dve_filled(rnd, *name):
            return before(DVE_IDX, rnd, name) + 1

        def act_has(rnd, *name):
            return before(ACT_IDX, rnd, name) + ACT_BANKS + 1

        def dve_has(rnd, *name):
            return before(DVE_IDX, rnd, name) + DVE_BANKS + 1

        def rows_view(t, r0, n):
            return t[:].rearrange("p w (r k) -> p r w k", k=K)[:, r0:r0 + n]

        with nc.Block() as block:
            @block.sync
            def _(sp):
                for dst, src in ((ident, w["ident"]), (block_ones, w["block_ones"]), (ones32, w["ones32"]),
                                 (eye32, w["eye32"]), (head_mask, w["head_mask"]), (dct_w, w["dct_w"]), (idct_w, w["idct_w"])):
                    sp.dma_start(dst[:], src).then_inc(consts_loaded, 16)
                sp.wait_ge(wts_zeroed, 1)
                for half in range(2):
                    r = slice(half * C, (half + 1) * C)
                    for i, name in enumerate(("c1a", "c2", "wv", "wq", "wk", "proj")):
                        sp.dma_start(wts[r, i, r], w[name]).then_inc(weights_loaded, 16)
                    sp.dma_start(tap_w[r, :], w["taps"]).then_inc(weights_loaded, 16)
                    sp.dma_start(bias[r, :], w["proj_b"].rearrange("(c n) -> c n", n=1)).then_inc(weights_loaded, 16)
                    for h in range(HEADS):
                        sp.dma_start(rescale[half * C + h * DH:half * C + (h + 1) * DH, :],
                                     w["rescale"][h:h + 1].partition_broadcast(DH)).then_inc(weights_loaded, 16)
                def load_y(s, b):
                    sp.wait_ge(act_full, (s * B + b) * ACT_TILES + 1)
                    sp.wait_ge(wts_zeroed, 1)
                    for q in range(2):
                        for half in range(2):
                            sp.dma_start(y_st[:, q, :, half, :],
                                         y_dram[b, bass.ds(s * K + half * P, ROWS), q]
                                         .rearrange("r w c -> w r c")).then_inc(y_loaded, 16)

                with sp.Fori(0, STRIPS) as s:
                    load_y(s, 0)
                    sp.wait_ge(dve_emptied, s * B * DVE_TILES + DVE_BANKS)
                    sp.wait_ge(wts_zeroed, 1)
                    for half in range(2):
                        sp.dma_start(coef[half * C:(half + 1) * C],
                                     w["coef"][bass.ds(s * K + half * P, K), :].rearrange("r w -> (r w)")
                                     .partition_broadcast(C)).then_inc(coef_loaded, 16)
                    with sp.Fori(1, B) as b:
                        load_y(s, b)

            @block.gpsimd
            def _(pool):
                nc.gpsimd.memset(wts[:], 0.0).then_inc(wts_zeroed, 1)
                nc.gpsimd.memset(spare[:], 0.0).then_inc(zeroed, 1)
                nc.gpsimd.memset(one[:], 1.0).then_inc(zeroed, 1)
                nc.gpsimd.memset(hi[:], 0.0).then_inc(hi_step, 1)
                nc.gpsimd.memset(base[:], 0.0).then_inc(base_step, 9)
                nc.gpsimd.memset(xc[:], 0.0).then_inc(xc_ready, 4)
                nc.gpsimd.memset(one_minus[:], 0.0).then_inc(zeroed, 1)
                nc.gpsimd.memset(z[:], 0.0).then_inc(zeroed, 1)
                nc.gpsimd.memset(out[:, 0, 0, 0, 0:1], 0.0).then_inc(z_stored, 1)
                pool.wait_ge(consts_loaded, 7 * 16)
                pool.wait_ge(weights_loaded, 24 * 16)
                pool.wait_ge(zeroed, 7)

                def x_conv(it, i):
                    pool.wait_ge(conv_emptied, it * 4 + CONV_BANKS + i + 1)
                    part = xc[:, 2 * i:2 * i + 2, :].rearrange("p r (w k) -> p r w k", k=K)
                    nc.gpsimd.tensor_tensor(part, part, rows_view(xd, 2 * i, 2), ALU.add).then_inc(xc_ready, 1)
                    rows = slice(2 * i, 2 * i + 2)
                    pool.wait_ge(xc_ready, it * 4 + 4 + i + 1)
                    nc.gpsimd.tensor_tensor(base[:, rows], xc[:, rows], one_minus[:, rows], ALU.mult
                                            ).then_inc(base_step, 1)
                    pool.wait_ge(base_step, it * 8 + 8 + 2 * i + 2)
                    part = base[:, rows, :].rearrange("p r (w k) -> p r w k", k=K)
                    nc.gpsimd.tensor_tensor(part, part, rows_view(xd, 2 * i, 2), ALU.add).then_inc(base_step, 1)

                def x_high(rnd, i):
                    rows = slice(2 * i, 2 * i + 2)
                    pool.wait_ge(act_emptied, act_has(rnd, "c2", i))
                    nc.gpsimd.tensor_tensor(hi[:, rows], hi[:, rows], one_minus[:, rows], ALU.mult
                                            ).then_inc(hi_step, 1)
                    pool.wait_ge(base_step, rnd * 8 + (9 if i == 3 else 8 + 2 * i + 3))
                    pool.wait_ge(hi_step, rnd * 8 + (2 if i == 3 else 2 * i + 4))
                    nc.gpsimd.tensor_tensor(hi[:, rows], hi[:, rows], base[:, rows], ALU.add
                                            ).then_inc(hi_step, 1)

                def strip(it):
                    x_conv(it, 0)
                    x_conv(it, 1)
                    pool.wait_ge(rnorm_ready, it + 1)
                    nc.gpsimd.tensor_tensor(diag_rk[:], rnorm[:, 1, :].unsqueeze(2).to_broadcast([P, 2 * T2, 32]),
                                            eye32[:].unsqueeze(1).to_broadcast([P, 2 * T2, 32]), ALU.mult
                                            ).then_inc(diag_ready, 1)
                    nc.gpsimd.tensor_scalar(rq[:], rnorm[:, 0, :], rescale[:, 0:1], None, ALU.mult
                                            ).then_inc(rq_ready, 1)
                    x_conv(it, 2)
                    x_high(it, 0)
                    x_high(it, 1)
                    x_conv(it, 3)
                    x_high(it, 2)

                with pool.Fori(0, STRIPS) as s:
                    first = pool.snap(s * B)
                    x_high(first, 3)
                    pool.wait_ge(coef_loaded, s * 32 + 32)
                    nc.gpsimd.tensor_tensor(one_minus[:].rearrange("p r w -> p (r w)"),
                                            one[:].to_broadcast([P, K * W]), coef[:].rearrange("p r w -> p (r w)"),
                                            ALU.subtract).then_inc(one_minus_ready, 1)
                    pool.wait_ge(one_minus_ready, s + 1)
                    strip(first)
                    with pool.Fori(1, B) as b:
                        it = pool.snap(s * B + b)
                        x_high(it, 3)
                        strip(it)
                x_high(LAST, 3)

            @block.scalar
            def _(act):
                act.wait_ge(zeroed, 7)
                nc.scalar.activation(row_sum[:], spare[:], ACT.Identity).then_inc(act_emptied, ACT_BANKS)
                nc.scalar.activation(row_inv[:], spare[:], ACT.Identity).then_inc(act_full, ACT_CREDIT)
                nc.scalar.activation(row_max[:], spare[:], ACT.Identity).then_inc(conv_emptied, CONV_BANKS)
                z_view = z_dram.rearrange("b q (g h) n c -> b q g n h c", g=2)

                def empty(rnd, out_ap, in_ap, func, *name, count=1):
                    act.wait_ge(act_full, act_filled(rnd, *name))
                    nc.scalar.activation(out_ap, in_ap, func).then_inc(act_emptied, count)

                def two_rows(bank):
                    return bank.rearrange("p (r w) -> p r w", r=2)

                def transposed(rnd):
                    for j in range(4):
                        empty(rnd, zt[:, j % 2, 4 * (j // 2):4 * (j // 2) + 4].rearrange("p r c -> p (r c)"),
                              act_bank(rnd, "t", j), ACT.Identity, "t", j)

                def inverse(rnd, tiles):
                    if 0 in tiles:
                        act.wait_ge(z_stored, rnd * 64 + 1)
                    for j in tiles:
                        rows = slice(4 * (j // 2), 4 * (j // 2) + 4)
                        empty(rnd, out[:, j % 2, :, rows, :].rearrange("p g r c -> p r g c"),
                              act_bank(rnd, "idct", j).rearrange("p (r g c) -> p r g c", r=4, g=2),
                              ACT.Identity, "idct", j)

                def store(rnd, b, s):
                    act.wait_ge(act_emptied, act_has(rnd, "idct", 3))
                    for q in range(2):
                        for half in range(2):
                            act.dma_start(z_view[b, q, half, :, bass.ds(s * K, K), :], out[:, q, half]
                                          ).then_inc(z_stored, 16)

                def c2(rnd, j):
                    empty(rnd, hi[:, 2 * j:2 * j + 2], two_rows(act_bank(rnd, "c2", j)), ACT.Gelu, "c2", j,
                          count=2 if j == 2 else 1)

                with act.Fori(0, LAST) as it:
                    c2(it, 3)
                    empty(it, xh[:], two_rows(act_bank(it, "dct", 0)), ACT.Identity, "dct", 0)
                    for j in range(4):
                        act.wait_ge(base_step, it * 8 + 2 * j + 3)
                        empty(it, rows_view(xd, 2 * j, 2),
                              act_bank(it, "dct", j + 1).rearrange("p (r w k) -> p r w k", r=2, k=K),
                              ACT.Identity, "dct", j + 1)
                    empty(it, h1[:, 0:ROWS:ROWS - 1, 1:W + 1], two_rows(act_bank(it, "c1", 0)), ACT.Gelu, "c1", 0)
                    for j in range(4):
                        empty(it, h1[:, 2 * j + 1:2 * j + 3, 1:W + 1], two_rows(act_bank(it, "c1", j + 1)), ACT.Gelu,
                              "c1", j + 1)

                    def q_and_k(j):
                        act.wait_ge(act_full, act_filled(it, "qk", j))
                        pairs = slice(2 * j, 2 * j + 2)
                        nc.scalar.activation(qk[:, pairs].rearrange("p a b c -> p (a b c)"), act_bank(it, "qk", j),
                                             ACT.Identity)
                        nc.scalar.activation(sq[:, pairs].rearrange("p a b c -> p (a b c)"), act_bank(it, "qk", j),
                                             ACT.Square).then_inc(act_emptied, 1)

                    def conv(i):
                        act.wait_ge(tap_step, it * DVE_TAPS + tap_steps(i + 1))
                        nc.scalar.activation(xc[:, 2 * i:2 * i + 2], two_rows(conv_bank(i)), ACT.Gelu
                                             ).then_inc(conv_emptied, 1)

                    def softmax_exp(b):
                        act.wait_ge(shifted, it * 2 + b + 1)
                        part = logits[:, b * T2:(b + 1) * T2]
                        nc.scalar.activation(part, part, ACT.Exp).then_inc(exp_ready, 1)

                    for j in range(4):
                        q_and_k(j)
                    conv(0)
                    for j in range(4, 8):
                        q_and_k(j)
                    conv(1)
                    def values(j):
                        empty(it, v[:, 8 * j:8 * j + 8].rearrange("p w k -> p (w k)"), act_bank(it, "v", j),
                              ACT.Identity, "v", j)

                    values(0)
                    values(1)
                    act.wait_ge(dve_emptied, dve_has(it, "norm", 0))
                    nc.scalar.activation(norm[:], norm[:], ACT.Sqrt).then_inc(rooted, 1)
                    values(2)
                    values(3)
                    conv(2)
                    softmax_exp(0)
                    transposed(it)
                    inverse(it, (0, 1))
                    softmax_exp(1)
                    inverse(it, (2, 3))
                    c2(it, 0)
                    c2(it, 1)
                    for j in range(4):
                        act.wait_ge(act_full, act_filled(it, "av", j))
                        first = 8 * j % T2 * 2 + j // 2
                        last = nc.scalar.activation(av[:, :, first:first + T2 - 1:2, :],
                                                    act_bank(it, "av", j).rearrange("p (n r k) -> p r n k", n=8, k=K),
                                                    ACT.Identity)
                        last.then_inc(act_emptied, 1)
                    c2(it, 2)
                    conv(3)
                    prev = (it + (LAST - 1)) % LAST
                    store(it, prev % B, prev // B)
                c2(LAST, 3)
                transposed(LAST)
                inverse(LAST, range(4))
                store(LAST, B - 1, STRIPS - 1)
                act.wait_ge(z_stored, (LAST + 1) * 64 + 1)

            @block.vector
            def _(dve):
                for tile in (attn, av, h1):
                    nc.vector.memset(tile[:], 0.0).then_inc(zeroed, 1)
                dve.wait_ge(consts_loaded, 7 * 16)
                dve.wait_ge(weights_loaded, 24 * 16)
                for t in range(TAPS):
                    nc.vector.tensor_scalar(taps[:, t, :], ident[:], tap_w[:, t:t + 1], None, ALU.mult
                                            ).then_inc(taps_ready, 1)
                nc.vector.memset(rnorm[:], 0.0).then_inc(dve_emptied, DVE_BANKS)

                def full(rnd, *name):
                    dve.wait_ge(dve_full, dve_filled(rnd, *name))

                def finish_z(rnd):
                    for r in range(2):
                        rows = slice(4 * r, 4 * r + 4)
                        dve.wait_ge(hi_step, rnd * 8 + 3)
                        nc.vector.tensor_tensor(z[:, rows], z[:, rows], hi[:, rows], ALU.add).then_inc(z_ready, 1)

                with dve.Fori(0, LAST) as it:
                    def add_taps(i):
                        bank = conv_bank(i).rearrange("p (r w) -> p r w", r=2)
                        dve.wait_ge(act_emptied, act_has(it, "c1", min(i + 2, 4)))
                        dve.wait_ge(conv_full, it * 4 + i + 1)
                        for n in range(TAPS - PE_TAPS[i]):
                            tap = PE_TAPS[i] + n
                            dr, dw = tap // 3, tap % 3
                            if n:
                                dve.wait_ge(tap_step, it * DVE_TAPS + tap_steps(i, n))
                            nc.vector.scalar_tensor_tensor(out=bank, in0=h1[:, 2 * i + dr:2 * i + dr + 2, dw:dw + W],
                                                           scalar=tap_w[:, tap:tap + 1], in1=bank,
                                                           op0=ALU.mult, op1=ALU.add).then_inc(tap_step, 1)

                    def make_logits(b):
                        blocks = slice(b * T2, (b + 1) * T2)
                        part = logits[:, blocks]
                        full(it, "s", b)
                        nc.vector.tensor_tensor(part, dve_bank(it, "s", b).rearrange("p (t e) -> p t e", e=32),
                                                rq[:, blocks].unsqueeze(2).to_broadcast([P, T2, 32]), ALU.mult
                                                ).then_inc(dve_emptied, 1)
                        full(it, "rk", b)
                        dve.wait_ge(dve_emptied, dve_has(it, "s", b))
                        nc.vector.tensor_tensor(part, dve_bank(it, "rk", b).rearrange("p (t e) -> p t e", e=32),
                                                part, ALU.mult).then_inc(dve_emptied, 1)
                        dve.wait_ge(dve_emptied, dve_has(it, "rk", b))
                        nc.vector.tensor_tensor(part, part, head_mask[:].unsqueeze(1).to_broadcast([P, T2, 32]),
                                                ALU.add).then_inc(masked, 1)
                        dve.wait_ge(masked, it * 2 + b + 1)
                        nc.vector.tensor_reduce(row_max[:, blocks], part, AX.X, ALU.max).then_inc(max_ready, 1)
                        dve.wait_ge(max_ready, it * 2 + b + 1)
                        nc.vector.tensor_tensor(part, part, row_max[:, blocks].unsqueeze(2).to_broadcast([P, T2, 32]),
                                                ALU.subtract).then_inc(shifted, 1)

                    def normalise(b):
                        blocks = slice(b * T2, (b + 1) * T2)
                        part = logits[:, blocks]
                        count = it * 2 + b + 1
                        dve.wait_ge(exp_ready, count)
                        nc.vector.tensor_reduce(row_sum[:, blocks], part, AX.X, ALU.add).then_inc(sum_ready, 1)
                        dve.wait_ge(sum_ready, count)
                        nc.vector.reciprocal(row_inv[:, blocks], row_sum[:, blocks]).then_inc(inv_ready, 1)
                        dve.wait_ge(inv_ready, count)
                        nc.vector.tensor_tensor(part, part, row_inv[:, blocks].unsqueeze(2).to_broadcast([P, T2, 32]),
                                                ALU.mult).then_inc(normed, 1)
                        dve.wait_ge(normed, count)
                        nc.vector.transpose(probs_t[:, blocks].rearrange("p t e -> p (t e)"),
                                            part.rearrange("p t e -> p (t e)")).then_inc(turned, 1)
                        dve.wait_ge(turned, count)
                        for j in range(4):
                            r = slice(32 * j, 32 * j + 32)
                            nc.vector.tensor_copy(attn[r, blocks, r], probs_t[r, blocks]).then_inc(attn_ready, 1)

                    add_taps(0)
                    finish_z(it)
                    add_taps(1)
                    add_taps(2)
                    full(it, "norm", 0)
                    nc.vector.tensor_scalar(norm[:].rearrange("p a b -> p (a b)"), dve_bank(it, "norm", 0)[:, 0:64],
                                            1e-24, None, ALU.max).then_inc(dve_emptied, 1)
                    dve.wait_ge(rooted, it + 1)
                    nc.vector.reciprocal(rnorm[:].rearrange("p a b -> p (a b)"), norm[:].rearrange("p a b -> p (a b)")
                                         ).then_inc(rnorm_ready, 1)
                    dve.wait_ge(rq_ready, it + 1)
                    make_logits(0)
                    make_logits(1)
                    normalise(0)
                    normalise(1)
                    add_taps(3)
                    for q in range(4):
                        part = slice(64 * q, 64 * q + 64)
                        full(it, "low", q)
                        nc.vector.scalar_tensor_tensor(out=z[:, :, part],
                                                       in0=dve_bank(it, "low", q).rearrange("p (r w) -> p r w", r=K),
                                                       scalar=bias[:, 0:1], in1=coef[:, :, part],
                                                       op0=ALU.add, op1=ALU.mult).then_inc(dve_emptied, 1)
                    dve.wait_ge(dve_emptied, dve_has(it, "low", 3))
                finish_z(LAST)

            @block.tensor
            def _(pe):
                pe.wait_ge(consts_loaded, 7 * 16)
                pe.wait_ge(weights_loaded, 24 * 16)
                pe.wait_ge(taps_ready, TAPS)
                pe.wait_ge(zeroed, 7)
                c1a_w, c2_w, v_w = (wts[:, i, :] for i in range(3))
                proj_w = wts[:, 5, :]
                qk_w = wts[:, 3:5, :].rearrange("p a b -> p (a b)")

                def act_tile(rnd, *name):
                    pe.wait_ge(act_emptied, before(ACT_IDX, rnd, name) + 1)
                    return act_bank(rnd, *name)

                def dve_tile(rnd, *name):
                    pe.wait_ge(dve_emptied, before(DVE_IDX, rnd, name) + 1)
                    return dve_bank(rnd, *name)

                def transpose_z(rnd):
                    for j in range(4):
                        pe.wait_ge(z_ready, rnd * 2 + j // 2 + 1)
                        bank = act_tile(rnd, "t", j)
                        for r in range(4):
                            last = nc.tensor.transpose(bank[:, r * P:(r + 1) * P],
                                                       z[:, 4 * (j // 2) + r, j % 2:W:2], ident[:])
                        last.then_inc(act_full, 1)

                def inverse_dct(rnd):
                    for j in range(4):
                        rows = slice(4 * (j // 2), 4 * (j // 2) + 4)
                        pe.wait_ge(act_emptied, act_has(rnd, "t", j))
                        nc.tensor.matmul(act_tile(rnd, "idct", j), idct_w[:, j % 2, :],
                                         zt[:, j % 2, rows].rearrange("p r c -> p (r c)"),
                                         start=True, stop=True).then_inc(act_full, 1)

                def c2(rnd, i):
                    pe.wait_ge(xc_ready, rnd * 4 + 4 + (0 if i == 3 else i + 1))
                    nc.tensor.matmul(act_tile(rnd, "c2", i), c2_w, xc[:, 2 * i:2 * i + 2, :],
                                     start=True, stop=True).then_inc(act_full, 2 if i == 2 else 1)

                with pe.Fori(0, LAST) as it:
                    def conv(i):
                        pe.wait_ge(act_emptied, act_has(it, "c1", min(i + 2, 4)))
                        pe.wait_ge(conv_emptied, it * 4 + i + 1)
                        bank = conv_bank(i)
                        for t in range(PE_TAPS[i]):
                            dr, dw = t // 3, t % 3
                            last = nc.tensor.matmul(bank, taps[:, t, :], h1[:, 2 * i + dr:2 * i + dr + 2, dw:dw + W],
                                                    start=(t == 0), stop=(t == PE_TAPS[i] - 1))
                        last.then_inc(conv_full, 1)

                    pe.wait_ge(y_loaded, it * 64 + 64)
                    c2(it, 3)
                    for j in range(5):
                        bank = act_tile(it, "dct", j)
                        for n, row in enumerate((0, ROWS - 1) if j == 0 else (2 * j - 1, 2 * j)):
                            for q in range(2):
                                last = nc.tensor.matmul(bank[:, n * W + q:(n + 1) * W:2],
                                                        y_st[:, q, row].rearrange("p g c -> p (g c)"), dct_w[:, q, :],
                                                        start=True, stop=True)
                        last.then_inc(act_full, 1)
                    def c1(j):
                        pe.wait_ge(act_emptied, act_has(it, "dct", j))
                        nc.tensor.matmul(act_tile(it, "c1", j), c1a_w, xh[:] if j == 0 else rows_view(xd, 2 * j - 2, 2),
                                         start=True, stop=True).then_inc(act_full, 1)

                    def q_and_k(j):
                        bank = act_tile(it, "qk", j)
                        for t in range(2):
                            pair = 2 * j + t
                            last = nc.tensor.matmul(bank[:, t * 256:(t + 1) * 256],
                                                    xd[:, 2 * pair:2 * pair + 2].rearrange("p w k -> p (w k)"), qk_w,
                                                    start=True, stop=True)
                        last.then_inc(act_full, 1)

                    def norms(j):
                        pe.wait_ge(act_emptied, act_has(it, "qk", j))
                        for t in (2 * j, 2 * j + 1):
                            for q in range(2):
                                last = nc.tensor.matmul(norm_bank[:, q, :, t], sq[:, t, q, :], block_ones[:],
                                                        start=True, stop=True)
                        return last

                    def values(j):
                        nc.tensor.matmul(act_tile(it, "v", j), v_w, xd[:, 8 * j:8 * j + 8].rearrange("p w k -> p (w k)"),
                                         start=True, stop=True).then_inc(act_full, 1)

                    def scores(b):
                        pos = slice(64 * b, 64 * b + 64)
                        for t in range(T2):
                            for g in range(4):
                                ch = slice(32 * g, 32 * g + 32)
                                last = nc.tensor.matmul(s_banks[b][ch, 32 * t:32 * t + 32], qk[pos, t, 0, ch],
                                                        qk[pos, t, 1, ch], start=True, stop=True)
                        last.then_inc(dve_full, 1)

                    def k_norms(b):
                        nc.tensor.matmul(dve_tile(it, "rk", b), ones32[:],
                                         diag_rk[:, b * T2:(b + 1) * T2].rearrange("p t e -> p (t e)"),
                                         start=True, stop=True).then_inc(dve_full, 1)

                    for j in range(4):
                        c1(j)
                    conv(0)
                    c1(4)
                    for j in range(4):
                        q_and_k(j)
                    conv(1)
                    norm_bank = dve_tile(it, "norm", 0)[:, 0:64].rearrange("p (q b t) -> p q b t", q=2, b=2)
                    for j in range(4, 8):
                        q_and_k(j)
                        norms(j - 4)
                    conv(2)
                    norms(4)
                    values(0)
                    norms(5)
                    values(1)
                    norms(6)
                    values(2)
                    norms(7).then_inc(dve_full, 1)
                    s_banks = [dve_tile(it, "s", 0)]
                    values(3)
                    scores(0)
                    conv(3)
                    pe.wait_ge(diag_ready, it + 1)
                    s_banks.append(dve_tile(it, "s", 1))
                    k_norms(0)
                    scores(1)
                    k_norms(1)
                    transpose_z(it)
                    inverse_dct(it)
                    c2(it, 0)
                    c2(it, 1)
                    for j in range(4):
                        pe.wait_ge(attn_ready, it * 8 + 4 * (j // 2) + 4)
                        bank = act_tile(it, "av", j)
                        for n in range(8):
                            block = 8 * j + n
                            last = nc.tensor.matmul(bank[:, n * C:(n + 1) * C], attn[:, block, :],
                                                    v[:, block % T2 * 2 + block // T2, :], start=True, stop=True)
                        last.then_inc(act_full, 1)
                    c2(it, 2)
                    pe.wait_ge(act_emptied, act_has(it, "av", 3))
                    for q in range(4):
                        nc.tensor.matmul(dve_tile(it, "low", q).rearrange("p (r w) -> p r w", r=K), proj_w,
                                         av[:, :, 8 * q:8 * q + 8, :].rearrange("p r n k -> p r (n k)"),
                                         start=True, stop=True).then_inc(dve_full, 1)
                c2(LAST, 3)
                transpose_z(LAST)
                inverse_dct(LAST)


def inverse_phase(nc, x, z_dram, idct, out, psum):
    with ExitStack() as ctx:
        def sb(name, shape):
            return ctx.enter_context(nc.sbuf_tensor("i_" + name, shape, F32))

        def sem(name):
            return ctx.enter_context(nc.semaphore("i_" + name))

        idct_h = sb("idct_h", [P, 2, H])
        z_sb = sb("z_sb", [P, SLOTS, 2, 2, WT * C])
        x_sb = sb("x_sb", [P, SLOTS, 2, 2, WT * C])
        o_sb = sb("o_sb", [P, SLOTS, 2, 2, WT * C])

        consts_loaded = sem("consts_loaded")
        z_loaded = [sem(f"z_loaded{i}") for i in range(SLOTS)]
        x_loaded = [sem(f"x_loaded{i}") for i in range(SLOTS)]
        psum_full = sem("psum_full")
        psum_used = sem("psum_used")
        added = sem("added")
        stored = [sem(f"stored{i}") for i in range(SLOTS)]
        x_view = x.rearrange("b (k p) g w c -> b p k g (w c)", p=P)
        z_view = z_dram.rearrange("b q h w c -> b q h (w c)")
        out_view = out.rearrange("b (k p) g w c -> b p k g (w c)", p=P)

        with nc.Block() as block:
            @block.sync
            def _(sp):
                sp.dma_start(idct_h[:], idct.rearrange("(k p) n -> p k n", p=P)).then_inc(consts_loaded, 16)
                with sp.Fori(0, B) as b:
                    with sp.Fori(0, I_STEPS) as i:
                        for slot in range(SLOTS):
                            sp.wait_ge(psum_used, (b * I_STEPS + i) * 2 * SLOTS + 2 * slot + 2)
                            sp.wait_ge(consts_loaded, 16)
                            for k in range(2):
                                for q in range(2):
                                    sp.dma_start(z_sb[:, slot, k, q],
                                                 z_view[b, q, k * P:(k + 1) * P,
                                                        bass.ds((i * SLOTS + slot) * WT * C, WT * C)]
                                                 ).then_inc(z_loaded[slot], 16)
                            for k in range(2):
                                sp.dma_start(x_sb[:, slot, k],
                                             x_view[b, :, k, :, bass.ds((i * SLOTS + slot) * WT * C, WT * C)]
                                             ).then_inc(x_loaded[slot], 16)

            @block.tensor
            def _(pe):
                pe.wait_ge(consts_loaded, 16)
                with pe.Fori(0, B * I_STEPS) as it:
                    for slot in range(SLOTS):
                        pe.wait_ge(z_loaded[slot], it * 64 + 64)
                        for m in range(2):
                            n = 2 * slot + m
                            pe.wait_ge(psum_used, (it + 1) * 2 * SLOTS + n - 3)
                            for q in range(2):
                                for k in range(2):
                                    last = nc.tensor.matmul(psum[:, 2 * (n % 4) + q, :], idct_h[:, k, m * P:(m + 1) * P],
                                                            z_sb[:, slot, k, q, :], start=(k == 0), stop=(k == 1))
                            last.then_inc(psum_full, 1)

            @block.vector
            def _(dve):
                nc.vector.memset(o_sb[:, 0, 0, 0, 0:2], 0.0).then_inc(psum_used, 2 * SLOTS)
                for slot in range(SLOTS):
                    nc.vector.memset(o_sb[:, slot, 1, 0, 0:2], 0.0).then_inc(stored[slot], 1)
                with dve.Fori(0, B * I_STEPS) as it:
                    for slot in range(SLOTS):
                        dve.wait_ge(x_loaded[slot], it * 32 + 32)
                        dve.wait_ge(stored[slot], it * 32 + 1)
                        for m in range(2):
                            n = 2 * slot + m
                            even, odd = psum[:, 2 * (n % 4), :], psum[:, 2 * (n % 4) + 1, :]
                            dve.wait_ge(psum_full, it * 2 * SLOTS + n + 1)
                            for g in range(2):
                                last = nc.vector.tensor_tensor(o_sb[:, slot, m, g], even, x_sb[:, slot, m, g], ALU.add)
                            last.then_inc(added, 1)
                            dve.wait_ge(added, it * 2 * SLOTS + n + 1)
                            for g, op in enumerate((ALU.add, ALU.subtract)):
                                last = nc.vector.tensor_tensor(o_sb[:, slot, m, g], o_sb[:, slot, m, g], odd, op)
                            last.then_inc(psum_used, 1)

            @block.scalar
            def _(act):
                with act.Fori(0, B) as b:
                    with act.Fori(0, I_STEPS) as i:
                        for slot in range(SLOTS):
                            act.wait_ge(psum_used, (b * I_STEPS + i + 1) * 2 * SLOTS + 2 * slot + 2)
                            for k in range(2):
                                act.dma_start(out_view[b, :, k, :, bass.ds((i * SLOTS + slot) * WT * C, WT * C)],
                                              o_sb[:, slot, k]).then_inc(stored[slot], 16)
                for slot in range(SLOTS):
                    act.wait_ge(stored[slot], B * I_STEPS * 32 + 1)


def build(nc, args, out):
    y_dram = nc.dram_tensor("y_dram", (B, H + 2, 2, HW, C), F32, kind="Internal").ap()
    z_dram = nc.dram_tensor("z_dram", (B, 2, H, HW, C), F32, kind="Internal").ap()
    with nc.psum_tensor("psum", [P, 8, BANK], F32) as psum:
        forward_phase(nc, args["x"], y_dram, args["dct"], args["group_avg"], psum)
        mix_phase(nc, y_dram, z_dram, args, psum)
        inverse_phase(nc, args["x"], z_dram, args["idct"], out, psum)


def shape_constants():
    import numpy as np

    n = np.arange(H)
    cos = np.cos(np.pi * (2 * n[None, :] + 1) * n[:, None] / (2 * H))
    wk = np.ones(H)
    wk[0] = 0.5
    dct = np.ascontiguousarray((2.0 * cos).T).astype(np.float32)
    idct = (wk[:, None] * cos / H).astype(np.float32)
    p = np.arange(P)
    return {
        "dct": dct,
        "idct": idct,
        "dct_w": dct[:HW].reshape(HW, HW, 2).transpose(0, 2, 1),
        "idct_w": idct[:, :HW].reshape(HW, 2, HW),
        "group_avg": ((p[:, None] // GROUP_ROWS == p[None, :] // GROUP_ROWS) / GROUP_ROWS).astype(np.float32),
        "ident": np.eye(P, dtype=np.float32),
        "block_ones": (p[:, None] // C == np.arange(2)[None, :]).astype(np.float32),
        "ones32": (p[:, None] // 32 == p[None, :] // 32).astype(np.float32),
        "eye32": (p[:, None] % 32 == np.arange(32)[None, :]).astype(np.float32),
        "head_mask": np.where(p[:, None] % 32 // DH == np.arange(32)[None, :] // DH, 0, -1e30).astype(np.float32),
    }


def kernel(x, L0_conv_Wq, L0_conv_Wk, L0_conv_Wv, L0_conv_rescale, L0_conv_proj_w, L0_conv_proj_b,
           L0_conv_c1a_w, L0_conv_c1b_w, L0_conv_c2_w, L0_conv_coef_emb):
    import numpy as np
    import concourse.bacc as bacc
    from concourse.bass_utils import run_bass_kernel_spmd

    def mirror(a):
        a = np.asarray(a).reshape(B, H, 2, HW, C)
        return np.stack([a[:, :, 0], a[:, :, 1, ::-1]], axis=2)

    arrays = {
        "x": mirror(x), "wq": L0_conv_Wq, "wk": L0_conv_Wk, "wv": L0_conv_Wv, "proj": L0_conv_proj_w,
        "proj_b": L0_conv_proj_b, "rescale": np.asarray(L0_conv_rescale).reshape(HEADS, 1),
        "c1a": np.asarray(L0_conv_c1a_w).reshape(C, C).T, "c2": np.asarray(L0_conv_c2_w).reshape(C, C).T,
        "taps": np.asarray(L0_conv_c1b_w).reshape(C, TAPS), "coef": L0_conv_coef_emb,
        **shape_constants(),
    }
    arrays = {name: np.ascontiguousarray(a) for name, a in arrays.items()}
    nc = bacc.Bacc("TRN2", target_bir_lowering=False, num_devices=1)
    args = {name: nc.dram_tensor(name, a.shape, mybir.dt.from_np(a.dtype), kind="ExternalInput").ap()
            for name, a in arrays.items()}
    out = nc.dram_tensor("result", (B, H, 2, HW, C), F32, kind="ExternalOutput").ap()
    build(nc, args, out)
    result = run_bass_kernel_spmd(nc, [arrays], core_ids=[0]).results[0]["result"]
    return mirror(result).reshape(B, H, W, C)
```
